# Optimizing a Trainium2 kernel written in Bass

```python
import numpy as np
import jax
import jax.numpy as jnp

def _softmax(x, axis=-1):
    return jax.nn.softmax(x, axis=axis)

def _gelu(x):
    return jax.nn.gelu(x, approximate=True)

def _silu(x):
    return jax.nn.silu(x)

def _sigmoid(x):
    return jax.nn.sigmoid(x)

def _layernorm(x, axis=-1, eps=1e-05):
    m = jnp.mean(x, axis=axis, keepdims=True)
    v = jnp.var(x, axis=axis, keepdims=True)
    return (x - m) / jnp.sqrt(v + eps)

def _scatter_add(tgt, idx, src, axis=0):
    return tgt.at[idx].add(src)

def _segment_sum(src, seg, n):
    return jax.ops.segment_sum(src, seg, n)
kernel_name = 'mk_gnn_resnorm_d1_gnn_r32_450faa'

def setup_inputs(seed: int=0):
    np.random.seed(seed)
    _w = jnp.asarray

    def _rec_inputs():
        import jax
        import jax.numpy as jnp
        _gk = jax.random.key(seed)
        x = -0.000202 + 1 * jax.random.normal(jax.random.fold_in(_gk, 1), (3125, 128), jnp.float32)
        _s = jax.random.randint(jax.random.fold_in(_gk, 2), (25000,), 0, 3125, jnp.int32)
        _d = jax.random.randint(jax.random.fold_in(_gk, 3), (25000,), 0, 3125, jnp.int32)
        _loop = jnp.arange(3125, dtype=jnp.int32)
        src = jnp.concatenate([_s, _d, _loop])
        dst = jnp.concatenate([_d, _s, _loop])
        _o = jnp.argsort(dst, stable=True)
        src = src[_o]
        dst = dst[_o]
        edge_attr_32 = -5.3897e-05 + 0.999841 * jax.random.normal(jax.random.fold_in(_gk, 12), (53125, 32), jnp.float32)
        return (x, src, dst, edge_attr_32)
    x, src, dst, edge_attr_32 = _rec_inputs()

    def _L0_gnn_setup():
        import jax, jax.numpy as jnp
        import numpy as np
        N = 50000
        E = 25000
        DN = 128
        DE = 32
        BN = 128
        H = 128
        DO = 128
        SLOPE = 0.2

        def _lrelu(x):
            return jax.nn.leaky_relu(x, SLOPE)
        key = jax.random.key(seed)
        ks = jax.random.split(key, 30)

        def w(k, i, o):
            return jax.random.normal(k, (i, o), jnp.float32) / np.float32(np.sqrt(i))

        def b(k, o):
            return jax.random.normal(k, (o,), jnp.float32) * 0.01
        node_feat = jax.random.normal(ks[0], (N, DN), jnp.float32)
        e_feat = jax.random.normal(ks[1], (E, DE), jnp.float32)
        src = jax.random.randint(ks[2], (E,), 0, N)
        dst = jax.random.randint(ks[3], (E,), 0, N)
        return {'node_feat': node_feat, 'e_feat': e_feat, 'src': src, 'dst': dst, 'We': w(ks[4], DE, BN), 'be': b(ks[5], BN), 'Ws': w(ks[6], DN, BN), 'bs': b(ks[7], BN), 'Wd': w(ks[8], DN, BN), 'bd': b(ks[9], BN), 'T1': w(ks[10], BN, BN), 'tb1': b(ks[11], BN), 'T2': w(ks[12], BN, BN), 'tb2': b(ks[13], BN), 'Wpd': w(ks[14], DN, H), 'bpd': b(ks[15], H), 'Wpe': w(ks[16], BN, H), 'bpe': b(ks[17], H), 'P1': w(ks[18], H, H), 'pb1': b(ks[19], H), 'P2': w(ks[20], H, H), 'pb2': b(ks[21], H), 'P3': w(ks[22], H, DO), 'pb3': b(ks[23], DO)}
    _L0_gnn_all = _L0_gnn_setup()
    _L0_gnn_in = {k: v for k, v in _L0_gnn_all.items() if k in ('We', 'be', 'Ws', 'bs', 'Wd', 'bd', 'T1', 'tb1', 'T2', 'tb2', 'Wpd', 'bpd', 'Wpe', 'bpe', 'P1', 'pb1', 'P2', 'pb2', 'P3', 'pb3')}
    del _L0_gnn_all
    return {'x': x, 'src': src, 'dst': dst, 'edge_attr_32': edge_attr_32, 'L0_gnn_We': _L0_gnn_in['We'], 'L0_gnn_be': _L0_gnn_in['be'], 'L0_gnn_Ws': _L0_gnn_in['Ws'], 'L0_gnn_bs': _L0_gnn_in['bs'], 'L0_gnn_Wd': _L0_gnn_in['Wd'], 'L0_gnn_bd': _L0_gnn_in['bd'], 'L0_gnn_T1': _L0_gnn_in['T1'], 'L0_gnn_tb1': _L0_gnn_in['tb1'], 'L0_gnn_T2': _L0_gnn_in['T2'], 'L0_gnn_tb2': _L0_gnn_in['tb2'], 'L0_gnn_Wpd': _L0_gnn_in['Wpd'], 'L0_gnn_bpd': _L0_gnn_in['bpd'], 'L0_gnn_Wpe': _L0_gnn_in['Wpe'], 'L0_gnn_bpe': _L0_gnn_in['bpe'], 'L0_gnn_P1': _L0_gnn_in['P1'], 'L0_gnn_pb1': _L0_gnn_in['pb1'], 'L0_gnn_P2': _L0_gnn_in['P2'], 'L0_gnn_pb2': _L0_gnn_in['pb2'], 'L0_gnn_P3': _L0_gnn_in['P3'], 'L0_gnn_pb3': _L0_gnn_in['pb3']}

def reference(x, src, dst, edge_attr_32, L0_gnn_We, L0_gnn_be, L0_gnn_Ws, L0_gnn_bs, L0_gnn_Wd, L0_gnn_bd, L0_gnn_T1, L0_gnn_tb1, L0_gnn_T2, L0_gnn_tb2, L0_gnn_Wpd, L0_gnn_bpd, L0_gnn_Wpe, L0_gnn_bpe, L0_gnn_P1, L0_gnn_pb1, L0_gnn_P2, L0_gnn_pb2, L0_gnn_P3, L0_gnn_pb3):
    import jax
    import jax.numpy as jnp

    def _L0_gnn_ref(node_feat, e_feat, src, dst, We, be, Ws, bs, Wd, bd, T1, tb1, T2, tb2, Wpd, bpd, Wpe, bpe, P1, pb1, P2, pb2, P3, pb3):
        import jax, jax.numpy as jnp
        import numpy as np
        N = 50000
        E = 25000
        DN = 128
        DE = 32
        BN = 128
        H = 128
        DO = 128
        SLOPE = 0.2

        def _lrelu(x):
            return jax.nn.leaky_relu(x, SLOPE)
        n = node_feat.shape[0]
        e_in = e_feat @ We + be + (node_feat[src] @ Ws + bs) + (node_feat[dst] @ Wd + bd)
        e_emb = _lrelu(e_in @ T1 + tb1) @ T2 + tb2
        message = jax.ops.segment_sum(e_emb, dst, num_segments=n)
        h = node_feat @ Wpd + bpd + (message @ Wpe + bpe)
        h = _lrelu(h) @ P1 + pb1
        h = _lrelu(h) @ P2 + pb2
        out = _lrelu(h) @ P3 + pb3
        return out
    x = _layernorm(x + _L0_gnn_ref(x, edge_attr_32, src, dst, L0_gnn_We, L0_gnn_be, L0_gnn_Ws, L0_gnn_bs, L0_gnn_Wd, L0_gnn_bd, L0_gnn_T1, L0_gnn_tb1, L0_gnn_T2, L0_gnn_tb2, L0_gnn_Wpd, L0_gnn_bpd, L0_gnn_Wpe, L0_gnn_bpe, L0_gnn_P1, L0_gnn_pb1, L0_gnn_P2, L0_gnn_pb2, L0_gnn_P3, L0_gnn_pb3), axis=-1)
    return x

_drawn_inputs = setup_inputs


def setup_inputs(seed=0):
    import zlib

    import numpy as np

    out = dict(_drawn_inputs(seed))
    spreads = {}
    factors = {'L0_gnn_be': 5.778,
     'L0_gnn_bs': 6.138,
     'L0_gnn_bd': 6.043,
     'L0_gnn_tb1': 7.046,
     'L0_gnn_tb2': 3.825,
     'L0_gnn_bpd': 64.0,
     'L0_gnn_bpe': 64.0,
     'L0_gnn_pb1': 54.045,
     'L0_gnn_pb2': 33.854,
     'L0_gnn_pb3': 23.27}
    for name, (base, spread) in spreads.items():
        noise = np.random.default_rng([zlib.crc32(name.encode()), seed]).standard_normal(out[name].shape)
        drawn = base * np.exp(spread * noise) if base else spread * noise
        out[name] = jnp.asarray(drawn.astype(out[name].dtype))
    for name, factor in factors.items():
        out[name] = (out[name] * factor).astype(out[name].dtype)
    return out
```

```python
from contextlib import ExitStack

import concourse.bass as bass
from concourse import mybir

F32 = mybir.dt.float32
I32 = mybir.dt.int32
ALU = mybir.AluOpType
ACT = mybir.ActivationFunctionType
AX = mybir.AxisListType

P = 128
NODES, EDGES, EDIM = 3125, 53125, 32
TILES = 4
GROUPS = 4
GROUP = TILES * P
STEPS = -(-EDGES // (GROUPS * GROUP))
NG = STEPS * GROUPS
SHIFT = 30
WIN = 96
SLAB = GROUPS * SHIFT
SPAN = SLAB - SHIFT + WIN
LEFT = NG // 2 * SHIFT + WIN // 2 - (NG + 1) * GROUP * NODES // (2 * EDGES)
SLABS = STEPS + 1
COLS = SLABS * SLAB
SLOPE = 0.2
EPS = 1e-5
CHUNK = 512
NCH = -(-COLS // CHUNK)

assert NODES + LEFT < SHIFT * (NG - 1) + WIN and NODES + LEFT < COLS

W_NAMES = ["WsT", "WdT", "T1", "T2T", "Wpe", "Wpd", "P1", "P2", "P3"]
B_NAMES = ["be", "bs", "bd", "tb2", "bpd", "bpe", "pb1", "pb2"]


def gnn_resnorm(nc, x, xT, srcT, dstT, eT, weights, WeT, bcols, brows, out):
    with ExitStack() as ctx:
        def sb(name, shape, dt=F32):
            return ctx.enter_context(nc.sbuf_tensor(name, shape, dt))

        def psum(name, shape):
            return ctx.enter_context(nc.psum_tensor(name, shape, F32))

        def sem(name):
            return ctx.enter_context(nc.semaphore(name))

        w_sb = sb("w_sb", [P, len(W_NAMES), P])
        wet_sb = sb("wet_sb", [P, EDIM])
        bc_sb = sb("bc_sb", [P, len(B_NAMES)])
        br_sb = sb("br_sb", [1, 2, P])
        xwin = sb("xwin", [P, GROUPS, WIN])
        xslab = sb("xslab", [P, SLAB])
        dst_i = sb("dst_i", [P, NG * TILES], I32)
        dst_f = sb("dst_f", [P, NG * TILES])
        rel = sb("rel", [P, NG, TILES])
        base_f = sb("base_f", [P, NG, TILES])
        bad = sb("bad", [P, NG * TILES])
        badsum = sb("badsum", [P, 1])
        flag = sb("flag", [1, 1], I32)
        iota_f = sb("iota_f", [P, CHUNK])
        ident = sb("ident", [P, P])
        ones = sb("ones", [P, P])
        bsum = sb("bsum", [P, 2])
        hbias = sb("hbias", [P, 1])
        eps_sb = sb("eps_sb", [P, 1])
        w_src = sb("w_src", [P, P])
        w_dst = sb("w_dst", [P, P])
        w_msg = sb("w_msg", [P, P])
        c_rows = sb("c_rows", [P, P])
        deg_w = sb("deg_w", [1, P])

        idx = sb("idx", [P, 2, 2 * TILES], I32)
        xg = sb("xg", [P, GROUPS, TILES, P])
        xgt = sb("xgt", [P, 2, GROUP])
        oh = sb("oh", [P, GROUPS, TILES, WIN])
        ohsum = sb("ohsum", [P, GROUPS, WIN])
        lhs = sb("lhs", [P, GROUPS, GROUP])
        rhs = sb("rhs", [P, GROUPS, P])
        h_low = sb("h_low", [P, 2, GROUP])
        h_sb = sb("h_sb", [P, 2, GROUP])
        macc = sb("macc", [P, SPAN])
        dacc = sb("dacc", [1, SPAN])
        mslab = sb("mslab", [P, SLAB])
        dslab = sb("dslab", [1, SLAB])
        hid_in = sb("hid_in", [P, 3, SLAB])
        hid = sb("hid", [P, 3, SLAB])
        stats = sb("stats", [SLAB, 6])
        mv = sb("mv", [SLAB, 2])
        sd = sb("sd", [SLAB, 1])
        rstd = sb("rstd", [SLAB, 1])
        y_raw = sb("y_raw", [SLAB, P])
        y_sb = sb("y_sb", [SLAB, P])

        gidx = sb("gidx", [P, 2, TILES], I32)
        gdst = sb("gdst", [P, TILES])
        gpre = sb("gpre", [P, P])
        goh = sb("goh", [P, CHUNK])
        mfull = sb("mfull", [P, NCH * CHUNK])
        dfull = sb("dfull", [1, NCH * CHUNK])

        ps_x = psum("ps_x", [P, 2, GROUP])
        ps_oh = psum("ps_oh", [P, GROUP])
        ps_h = psum("ps_h", [P, 2, GROUP])
        ps_m = psum("ps_m", [P, 2, GROUP // 2])
        ps_w = psum("ps_w", [P, GROUP])
        ps_l = psum("ps_l", [P, GROUP])

        w_in, dst_in, b_in = sem("w_in"), sem("dst_in"), sem("b_in")
        xwin_in = [sem(f"xwin_in{g}") for g in range(GROUPS)]
        xslab_in = sem("xslab_in")
        iota_done = sem("iota_done")
        ident_zero, ident_done, ones_done = sem("ident_zero"), sem("ident_done"), sem("ones_done")
        bias_done = sem("bias_done")
        setup_mm, setup_copied = sem("setup_mm"), sem("setup_copied")
        rel_step, bad_done, flag_mm, flag_done = sem("rel_step"), sem("bad_done"), sem("flag_mm"), sem("flag_done")
        acc_clear = sem("acc_clear")
        idx_in = [sem(f"idx_in{h}") for h in range(2)]
        gathered = [sem(f"gathered{g}") for g in range(GROUPS)]
        e_in = [sem(f"e_in{g}") for g in range(GROUPS)]
        xg_turned, xg_copied = sem("xg_turned"), sem("xg_copied")
        oh_ready, ohsum_ready = sem("oh_ready"), sem("ohsum_ready")
        oh_turned, oh_copied = sem("oh_turned"), sem("oh_copied")
        win_mm, win_ready = sem("win_mm"), sem("win_ready")
        pre_done, h_scaled, h_ready = sem("pre_done"), sem("h_scaled"), sem("h_ready")
        seg_done, m_added = sem("seg_done"), sem("m_added")
        acc_moved, slab_ready = sem("acc_moved"), sem("slab_ready")
        layer_mm, layer_biased, layer_act = sem("layer_mm"), sem("layer_biased"), sem("layer_act")
        stats_done, var_done, sd_done, rstd_done = sem("stats_done"), sem("var_done"), sem("sd_done"), sem("rstd_done")
        y_ready, y_out = sem("y_ready"), sem("y_out")
        g_in, g_gath, g_turned, g_copied = sem("g_in"), sem("g_gath"), sem("g_turned"), sem("g_copied")
        g_pre, g_added, g_h = sem("g_pre"), sem("g_added"), sem("g_h")
        g_dst, g_oh, g_mm, g_acc = sem("g_dst"), sem("g_oh"), sem("g_mm"), sem("g_acc")
        g_clear = sem("g_clear")

        def W(name):
            return w_sb[:, W_NAMES.index(name), :]

        def B(name, n=1):
            k = B_NAMES.index(name)
            return bc_sb[:, k:k + n]

        def wait(eng, s, value):
            if not isinstance(value, int) or value > 0:
                eng.wait_ge(s, value)

        block = ctx.enter_context(nc.Block())

        @block.sync
        def _(sp):
            def load_idx(i, half):
                for g in (2 * half, 2 * half + 1):
                    wait(sp, gathered[g], 16 * TILES * i)
                c = (i * (GROUPS * TILES)) + half * 2 * TILES
                sp.dma_start(idx[:, half, :], srcT[:, bass.ds(c, 2 * TILES)]).then_inc(idx_in[half], 16)

            def load_xslab(s, col):
                wait(sp, layer_mm, s * 4)
                sp.dma_start(xslab[:, :], xT[:, bass.ds(col, SLAB)]).then_inc(xslab_in, 16)

            def load_group(i, g):
                n = i * GROUPS + g
                wait(sp, win_mm, n - GROUPS + 1)
                sp.dma_start(xwin[:, g, :], xT[:, bass.ds(i * SLAB + g * SHIFT, WIN)]).then_inc(xwin_in[g], 16)
                wait(sp, pre_done, n - GROUPS + 1)
                sp.dma_start(lhs[WIN:P, g, :], eT[n]).then_inc(e_in[g], 16)

            def step(i, first, last):
                load_group(i, 0)
                load_idx(i, 1)
                load_group(i, 1)
                if not first:
                    load_xslab(i - 1, (i - 1) * SLAB)
                load_group(i, 2)
                if not last:
                    load_idx(i + 1, 0)
                load_group(i, 3)

            load_idx(0, 0)
            sp.dma_start(w_sb[:, :, :], weights).then_inc(w_in, 16)
            sp.dma_start(dst_i[:, :], dstT).then_inc(dst_in, 16)
            sp.dma_start(wet_sb[:, :], WeT).then_inc(b_in, 16)
            sp.dma_start(bc_sb[:, :], bcols).then_inc(b_in, 16)
            sp.dma_start(br_sb[:, :, :], brows).then_inc(b_in, 16)
            step(0, True, False)
            step(1, False, False)
            with sp.Fori(2, STEPS - 1) as i:
                step(i, False, False)
            step(STEPS - 1, False, True)
            for s in range(STEPS - 1, SLABS):
                load_xslab(s, s * SLAB)

            sp.wait_ge(flag_done, 1)
            wrong = sp.value_load(flag[0:1, 0:1], min_val=0, max_val=NG * GROUP)
            with sp.If(wrong > 0):
                def general_group(n):
                    wait(sp, g_mm, n * (TILES * NCH))
                    sp.dma_start(gidx[:, 0, :], srcT[:, bass.ds(n * TILES, TILES)]).then_inc(g_in, 16)
                    sp.dma_start(gidx[:, 1, :], dstT[:, bass.ds(n * TILES, TILES)]).then_inc(g_in, 16)
                    sp.dma_start(lhs[WIN:P, 0, :], eT[n]).then_inc(g_in, 16)

                general_group(0)
                with sp.Fori(1, NG) as n:
                    general_group(n)
                with sp.Fori(0, SLABS) as s:
                    load_xslab(s + SLABS, s * SLAB)

        @block.gpsimd
        def _(pool):
            bound, zero = pool.alloc_register("bound"), pool.alloc_register("nothing")
            pool.reg_mov(zero, 0)

            def gather(i, g):
                n = i * GROUPS + g
                wait(pool, xg_turned, n - GROUPS + 1)
                if g % 2 == 0:
                    pool.wait_ge(idx_in[g // 2], (i + 1) * 16)
                pool.reg_add(bound, zero, NODES - 1)
                for j in range(TILES):
                    col = (g % 2) * TILES + j
                    pool.indirect_dma_start(
                        out=xg[:, g, j, :], out_offset=None, in_=x[:, :],
                        in_offset=bass.IndirectOffsetOnAxis(ap=idx[:, g // 2, col:col + 1], axis=0),
                        bounds_check=bound, oob_is_err=True).then_inc(gathered[g], 16)

            pool.iota(iota_f[:, :], [[1, CHUNK]], base=0, channel_multiplier=0,
                      allow_small_or_imprecise_dtypes=True).then_inc(iota_done, 1)
            pool.iota(base_f[:, :, :], [[SHIFT, NG], [0, TILES]], base=0, channel_multiplier=0,
                      allow_small_or_imprecise_dtypes=True).then_inc(iota_done, 1)
            pool.memset(ident[:, :], 0.0).then_inc(ident_zero, 1)
            pool.wait_ge(ident_zero, 1)
            pool.affine_select(out=ident[:, :], in_=ident[:, :], compare_op=ALU.not_equal, fill=1.0,
                               base=0, pattern=[[-1, P]], channel_multiplier=1).then_inc(ident_done, 1)
            for g in range(GROUPS):
                gather(0, g)
            for g in range(GROUPS):
                gather(1, g)
            with pool.Fori(2, STEPS) as i:
                for g in range(GROUPS):
                    gather(i, g)

            pool.wait_ge(flag_done, 1)
            wrong = pool.value_load(flag[0:1, 0:1], min_val=0, max_val=NG * GROUP)
            with pool.If(wrong > 0):
                def general_gathers(n):
                    pool.wait_ge(g_in, (n + 1) * 48)
                    wait(pool, g_turned, n * TILES)
                    pool.reg_add(bound, zero, NODES - 1)
                    for side in range(2):
                        for j in range(TILES):
                            pool.indirect_dma_start(
                                out=xg[:, side, j, :], out_offset=None, in_=x[:, :],
                                in_offset=bass.IndirectOffsetOnAxis(ap=gidx[:, side, j:j + 1], axis=0),
                                bounds_check=bound, oob_is_err=True).then_inc(g_gath, 16)

                general_gathers(0)
                with pool.Fori(1, NG) as n:
                    general_gathers(n)

        @block.tensor
        def _(pe):
            pe.wait_ge(w_in, 16)
            pe.wait_ge(b_in, 48)
            pe.wait_ge(bias_done, 1)
            pe.wait_ge(ones_done, 1)
            pe.matmul(ps_x[:, 0, 0:P], W("WsT"), W("T1"), start=True, stop=True).then_inc(setup_mm, 1)
            pe.matmul(ps_x[:, 0, P:2 * P], W("WdT"), W("T1"), start=True, stop=True).then_inc(setup_mm, 1)
            pe.matmul(ps_x[:, 0, 2 * P:3 * P], W("T2T"), W("Wpe"), start=True, stop=True).then_inc(setup_mm, 1)
            pe.matmul(ps_x[:, 1, 0:P], bsum[:, 1:2].to_broadcast([P, P]), W("T1"), start=True, stop=False)
            pe.matmul(ps_x[:, 1, 0:P], ones[0:1, :], br_sb[0:1, 0, :], start=False, stop=True).then_inc(setup_mm, 1)
            pe.matmul(ps_x[0:1, 1, P:2 * P], B("tb2"), W("Wpe"), start=True, stop=True).then_inc(setup_mm, 1)
            pe.matmul(ps_h[WIN:P, 0, 0:P], wet_sb[:, :], W("T1"), start=True, stop=True).then_inc(setup_mm, 1)
            pe.wait_ge(bad_done, 1)
            pe.matmul(ps_m[0:1, 0, 0:1], badsum[:, :], ones[:, 0:1], start=True, stop=True).then_inc(flag_mm, 1)
            pe.wait_ge(flag_done, 1)
            pe.wait_ge(setup_copied, 9)
            pe.wait_ge(ident_done, 1)

            def window(i, g):
                n = i * GROUPS + g
                wait(pe, win_ready, n)
                pe.wait_ge(xwin_in[g], (i + 1) * 16)
                pe.matmul(ps_w[0:WIN, 0:P], xwin[:, g, :], w_dst[:, :],
                          start=True, stop=True).then_inc(win_mm, 1)

            def turn(i, g):
                n = i * GROUPS + g
                pe.wait_ge(oh_ready, n + 1)
                wait(pe, oh_copied, n)
                for j in range(TILES):
                    mm = pe.transpose(ps_oh[0:WIN, j * P:(j + 1) * P], oh[:, g, j, :], ident[:, :])
                mm.then_inc(oh_turned, 1)
                pe.wait_ge(gathered[g], (i + 1) * (16 * TILES))
                wait(pe, xg_copied, n - 1)
                for j in range(TILES):
                    mm = pe.transpose(ps_x[:, g % 2, j * P:(j + 1) * P], xg[:, g, j, :], ident[:, :])
                mm.then_inc(xg_turned, 1)

            def pre(i, g):
                n = i * GROUPS + g
                pe.wait_ge(xg_copied, n + 1)
                pe.wait_ge(oh_copied, n + 1)
                pe.wait_ge(win_ready, n + 1)
                pe.wait_ge(e_in[g], (i + 1) * 16)
                wait(pe, h_ready, n - 1)
                for j in range(TILES):
                    c = slice(j * P, (j + 1) * P)
                    pe.matmul(ps_h[:, g % 2, c], xgt[:, g % 2, c], w_src[:, :], start=True, stop=False)
                    mm = pe.matmul(ps_h[:, g % 2, c], lhs[:, g, c], rhs[:, g, :], start=False, stop=True)
                mm.then_inc(pre_done, 1)

            def seg(i, g):
                n = i * GROUPS + g
                pe.wait_ge(h_ready, n + 1)
                pe.wait_ge(ohsum_ready, n + 1)
                wait(pe, m_added, n)
                for j in range(TILES):
                    pe.matmul(ps_m[:, 0, 0:WIN], h_sb[:, g % 2, j * P:(j + 1) * P], oh[:, g, j, :],
                              start=(j == 0), stop=(j == TILES - 1))
                pe.matmul(ps_m[0:1, 1, 0:WIN], ones[:, 0:1], ohsum[:, g, :],
                          start=True, stop=True).then_inc(seg_done, 1)

            def layer(s, k):
                o = ps_l[:, 0:SLAB]
                if k == 0:
                    wait(pe, y_ready, s)
                    pe.wait_ge(slab_ready, s + 1)
                    pe.wait_ge(xslab_in, s * 16 + 16)
                    pe.matmul(o, W("Wpd"), xslab[:, :], start=True, stop=False)
                    pe.matmul(o, w_msg[:, :], mslab[:, :], start=False, stop=False)
                    pe.matmul(o, deg_w[0:1, :], dslab[0:1, :], start=False, stop=True).then_inc(layer_mm, 1)
                elif k < 3:
                    pe.wait_ge(layer_act, s * 3 + k)
                    pe.matmul(o, W(f"P{k}"), hid[:, k - 1, :], start=True, stop=True).then_inc(layer_mm, 1)
                else:
                    pe.wait_ge(layer_act, s * 3 + 3)
                    o = ps_l[0:SLAB, 0:P]
                    pe.matmul(o, hid[:, 2, :], W("P3"), start=True, stop=False)
                    pe.matmul(o, ones[0:1, 0:SLAB], br_sb[0:1, 1, :], start=False, stop=False)
                    pe.matmul(o, xslab[:, :], ident[:, :], start=False, stop=True).then_inc(layer_mm, 1)

            def step(i, first):
                for g in range(GROUPS):
                    window(i, g)
                    turn(i, g)
                    if g >= 2 and not first:
                        layer(i - 1, 2 * (g - 2))
                    if g >= 1:
                        pre(i, g - 1)
                    elif not first:
                        pre(i - 1, GROUPS - 1)
                    if g >= 2 and not first:
                        layer(i - 1, 2 * (g - 2) + 1)
                    if g >= 2:
                        seg(i, g - 2)
                    elif not first:
                        seg(i - 1, g + GROUPS - 2)

            step(0, True)
            step(1, False)
            with pe.Fori(2, STEPS) as i:
                step(i, False)
            pre(STEPS - 1, GROUPS - 1)
            seg(STEPS - 1, GROUPS - 2)
            seg(STEPS - 1, GROUPS - 1)
            for s in range(STEPS - 1, SLABS):
                for k in range(4):
                    layer(s, k)

            wrong = pe.value_load(flag[0:1, 0:1], min_val=0, max_val=NG * GROUP)
            with pe.If(wrong > 0):
                def general_group(n):
                    pe.wait_ge(g_gath, (n + 1) * (32 * TILES))
                    pe.wait_ge(g_in, (n + 1) * 48)
                    for j in range(TILES):
                        m = n * TILES + j
                        wait(pe, g_copied, m)
                        pe.transpose(ps_x[:, 0, 0:P], xg[:, 0, j, :], ident[:, :])
                        pe.transpose(ps_x[:, 0, P:2 * P], xg[:, 1, j, :], ident[:, :]).then_inc(g_turned, 1)
                        pe.wait_ge(g_copied, m + 1)
                        pe.matmul(ps_h[:, 0, 0:P], xgt[:, 0, 0:P], w_src[:, :], start=True, stop=False)
                        pe.matmul(ps_h[:, 0, 0:P], xgt[:, 0, P:2 * P], w_dst[:, :], start=False, stop=False)
                        pe.matmul(ps_h[:, 0, 0:P], lhs[WIN:P, 0, j * P:(j + 1) * P], rhs[WIN:P, 0, :],
                                  start=False, stop=True).then_inc(g_pre, 1)
                        pe.wait_ge(g_h, m + 1)
                        for c in range(NCH):
                            k = m * NCH + c
                            pe.wait_ge(g_oh, k + 1)
                            wait(pe, g_acc, k)
                            pe.matmul(ps_x[:, 1, :], h_sb[:, 0, 0:P], goh[:, :], start=True, stop=True)
                            pe.matmul(ps_h[0:1, 1, :], ones[:, 0:1], goh[:, :], start=True,
                                      stop=True).then_inc(g_mm, 1)

                general_group(0)
                with pe.Fori(1, NG) as n:
                    general_group(n)
                with pe.Fori(0, SLABS) as s:
                    for k in range(4):
                        layer(s + SLABS, k)

        @block.scalar
        def _(act):
            def copy_x(i, g):
                n = i * GROUPS + g
                act.wait_ge(xg_turned, n + 1)
                wait(act, pre_done, n - 1)
                act.activation(xgt[:, g % 2, :], ps_x[:, g % 2, :], ACT.Copy).then_inc(xg_copied, 1)

            def scale(i, g):
                n = i * GROUPS + g
                act.wait_ge(pre_done, n + 1)
                wait(act, h_ready, n - 1)
                act.activation(h_low[:, g % 2, :], ps_h[:, g % 2, :], ACT.Copy, scale=SLOPE).then_inc(h_scaled, 1)

            def layer_out(s, k):
                act.wait_ge(layer_mm, s * 4 + (k + 1))
                b = [hbias[:, :], B("pb1"), B("pb2")][k]
                act.activation(hid_in[:, k, :], ps_l[:, 0:SLAB], ACT.Identity,
                               bias=b).then_inc(layer_biased, 1)

            def deviation(s):
                act.wait_ge(var_done, s + 1)
                act.activation(sd[:, :], mv[:, 1:2], ACT.Sqrt, bias=eps_sb[0:SLAB, :]).then_inc(sd_done, 1)

            def step(i, first, second):
                for g in range(GROUPS):
                    copy_x(i, g)
                    if g == 1 and not first and not second:
                        store(i - 2)
                    if g >= 2 and not first:
                        layer_out(i - 1, 2 * (g - 2))
                    if g >= 1:
                        scale(i, g - 1)
                    elif not first:
                        scale(i - 1, GROUPS - 1)
                    if g == 2 and not first:
                        layer_out(i - 1, 1)
                if not first:
                    deviation(i - 1)

            def store(s, before=0):
                act.wait_ge(y_ready, s + (before + 1))
                act.dma_start(out[bass.ds(s * SLAB, SLAB), :], y_sb[:, :]).then_inc(y_out, 16)

            act.wait_ge(bias_done, 3)
            step(0, True, False)
            step(1, False, True)
            with act.Fori(2, STEPS) as i:
                step(i, False, False)
            scale(STEPS - 1, GROUPS - 1)
            store(STEPS - 2)
            for s in range(STEPS - 1, SLABS):
                for k in range(3):
                    layer_out(s, k)
                deviation(s)
                store(s)
            act.wait_ge(y_out, 16 * SLABS)

            act.wait_ge(flag_done, 1)
            wrong = act.value_load(flag[0:1, 0:1], min_val=0, max_val=NG * GROUP)
            with act.If(wrong > 0):
                def general_tile(m):
                    act.wait_ge(g_turned, m + 1)
                    act.activation(xgt[:, 0, 0:2 * P], ps_x[:, 0, 0:2 * P], ACT.Copy).then_inc(g_copied, 1)

                general_tile(0)
                with act.Fori(1, NG * TILES) as m:
                    general_tile(m)
                with act.Fori(0, SLABS) as s:
                    for k in range(3):
                        layer_out(s + SLABS, k)
                    deviation(s + SLABS)
                    store(s, SLABS)
                act.wait_ge(y_out, 32 * SLABS)

        @block.vector
        def _(dve):
            dve.memset(ones[:, :], 1.0).then_inc(ones_done, 1)
            dve.memset(eps_sb[:, :], EPS)
            dve.memset(macc[:, :], 0.0).then_inc(acc_clear, 1)
            dve.memset(dacc[:, :], 0.0).then_inc(acc_clear, 1)
            dve.wait_ge(b_in, 48)
            dve.tensor_tensor(bsum[:, 0:1], B("be"), B("bs"), ALU.add).then_inc(setup_copied, 1)
            dve.wait_ge(setup_copied, 1)
            dve.tensor_tensor(bsum[:, 1:2], bsum[:, 0:1], B("bd"), ALU.add).then_inc(bias_done, 1)
            dve.tensor_tensor(hbias[:, :], B("bpd"), B("bpe"), ALU.add).then_inc(bias_done, 2)
            dve.wait_ge(dst_in, 16)
            dve.tensor_scalar(dst_f[:, :], dst_i[:, :], float(LEFT), None, ALU.add).then_inc(rel_step, 1)
            dve.wait_ge(rel_step, 1)
            dve.wait_ge(iota_done, 2)
            relv = rel[:, :, :].rearrange("p n j -> p (n j)")
            dve.tensor_tensor(relv, dst_f[:, :], base_f[:, :, :].rearrange("p n j -> p (n j)"),
                              ALU.subtract).then_inc(rel_step, 1)
            dve.wait_ge(rel_step, 2)
            dve.tensor_scalar(bad[:, :], relv, 0.0, None, ALU.is_lt).then_inc(rel_step, 1)
            dve.wait_ge(rel_step, 3)
            dve.scalar_tensor_tensor(out=bad[:, :], in0=relv, scalar=float(WIN - 1), in1=bad[:, :],
                                     op0=ALU.is_gt, op1=ALU.add).then_inc(rel_step, 1)
            dve.wait_ge(rel_step, 4)
            dve.tensor_reduce(badsum[:, :], bad[:, :], AX.X, ALU.add).then_inc(bad_done, 1)
            dve.wait_ge(setup_mm, 6)
            dve.tensor_copy(w_src[:, :], ps_x[:, 0, 0:P]).then_inc(setup_copied, 1)
            dve.tensor_copy(w_dst[:, :], ps_x[:, 0, P:2 * P]).then_inc(setup_copied, 1)
            dve.tensor_copy(w_msg[:, :], ps_x[:, 0, 2 * P:3 * P]).then_inc(setup_copied, 1)
            dve.tensor_copy(c_rows[:, :], ps_x[:, 1, 0:P]).then_inc(setup_copied, 1)
            dve.tensor_copy(deg_w[0:1, :], ps_x[0:1, 1, P:2 * P]).then_inc(setup_copied, 1)
            for g in range(GROUPS):
                cp = dve.tensor_copy(rhs[WIN:P, g, :], ps_h[WIN:P, 0, 0:P])
                if g < 3:
                    cp.then_inc(setup_copied, 1)
                else:
                    cp.then_inc(acc_clear, 1)
            dve.wait_ge(flag_mm, 1)
            dve.tensor_copy(flag[:, :], ps_m[0:1, 0, 0:1]).then_inc(flag_done, 1)
            dve.wait_ge(acc_clear, 3)
            dve.wait_ge(setup_copied, 9)

            def one_hot(i, g):
                n = i * GROUPS + g
                wait(dve, seg_done, n - GROUPS + 1)
                dve.tensor_tensor(
                    oh[:, g, :, :], iota_f[:, None, 0:WIN].to_broadcast([P, TILES, WIN]),
                    rel[:, bass.ds(n, 1), :].rearrange("p a j -> p (a j)")[:, :, None].to_broadcast([P, TILES, WIN]),
                    ALU.is_equal).then_inc(oh_ready, 1)
                dve.wait_ge(oh_ready, n + 1)
                dve.tensor_reduce(ohsum[:, g, :], oh[:, g, :, :].rearrange("p j w -> p w j"), AX.X,
                                  ALU.add).then_inc(ohsum_ready, 1)

            def operands(i, g):
                n = i * GROUPS + g
                dve.wait_ge(win_mm, n + 1)
                wait(dve, pre_done, n - GROUPS + 1)
                dve.tensor_tensor(rhs[0:WIN, g, :], ps_w[0:WIN, 0:P], c_rows[0:WIN, :],
                                  ALU.add).then_inc(win_ready, 1)
                dve.wait_ge(oh_turned, n + 1)
                dve.tensor_copy(lhs[0:WIN, g, :], ps_oh[0:WIN, :]).then_inc(oh_copied, 1)

            def hidden(i, g):
                n = i * GROUPS + g
                dve.wait_ge(h_scaled, n + 1)
                wait(dve, seg_done, n - 1)
                dve.tensor_tensor(h_sb[:, g % 2, :], ps_h[:, g % 2, :], h_low[:, g % 2, :], ALU.max).then_inc(h_ready, 1)

            def layer_out(s, k):
                dve.wait_ge(layer_biased, s * 3 + (k + 1))
                dve.scalar_tensor_tensor(out=hid[:, k, :], in0=hid_in[:, k, :], scalar=SLOPE, in1=hid_in[:, k, :],
                                         op0=ALU.mult, op1=ALU.max).then_inc(layer_act, 1)

            def add_sums(i, g, moves):
                n = i * GROUPS + g
                dve.wait_ge(seg_done, n + 1)
                wait(dve, acc_moved, moves * 2)
                wait(dve, m_added, n)
                o = g * SHIFT
                dve.tensor_tensor(macc[:, o:o + WIN], macc[:, o:o + WIN], ps_m[:, 0, 0:WIN], ALU.add)
                dve.tensor_tensor(dacc[:, o:o + WIN], dacc[:, o:o + WIN], ps_m[0:1, 1, 0:WIN],
                                  ALU.add).then_inc(m_added, 1)

            def close_slab(s):
                dve.wait_ge(m_added, (s + 1) * GROUPS)
                wait(dve, layer_mm, s * 4)
                dve.tensor_copy(mslab[:, :], macc[:, 0:SLAB])
                dve.tensor_copy(dslab[:, :], dacc[:, 0:SLAB]).then_inc(slab_ready, 1)
                dve.wait_ge(slab_ready, s + 1)
                dve.tensor_copy(macc[:, 0:SPAN - SLAB], macc[:, SLAB:SPAN])
                dve.tensor_copy(dacc[:, 0:SPAN - SLAB], dacc[:, SLAB:SPAN]).then_inc(acc_moved, 1)
                dve.wait_ge(acc_moved, s * 2 + 1)
                dve.memset(macc[:, SPAN - SLAB:SPAN], 0.0)
                dve.memset(dacc[:, SPAN - SLAB:SPAN], 0.0).then_inc(acc_moved, 1)

            def normalize(s):
                y = ps_l[0:SLAB, 0:P]
                dve.wait_ge(layer_mm, s * 4 + 4)
                dve.bn_stats(stats[:, :], y).then_inc(stats_done, 1)
                dve.wait_ge(stats_done, s + 1)
                dve.tensor_copy(y_raw[:, :], y)
                dve.bn_aggr(mv[:, :], stats[:, :]).then_inc(var_done, 1)
                dve.wait_ge(sd_done, s + 1)
                dve.reciprocal(rstd[:, :], sd[:, :]).then_inc(rstd_done, 1)
                dve.wait_ge(rstd_done, s + 1)
                wait(dve, y_out, s * 16)
                dve.tensor_scalar(y_sb[:, :], y_raw[:, :], mv[:, 0:1], rstd[:, 0:1], ALU.subtract,
                                  ALU.mult).then_inc(y_ready, 1)

            def step(i, first):
                for g in range(GROUPS):
                    one_hot(i, g)
                    operands(i, g)
                    if g >= 2 and not first:
                        layer_out(i - 1, 2 * (g - 2))
                    if g >= 1:
                        hidden(i, g - 1)
                    elif not first:
                        hidden(i - 1, GROUPS - 1)
                    if g == 2 and not first:
                        layer_out(i - 1, 1)
                    if g >= 2:
                        add_sums(i, g - 2, i)
                    elif not first:
                        add_sums(i - 1, g + GROUPS - 2, i - 1)
                    if g == 1 and not first:
                        close_slab(i - 1)
                if not first:
                    normalize(i - 1)

            step(0, True)
            step(1, False)
            with dve.Fori(2, STEPS) as i:
                step(i, False)
            hidden(STEPS - 1, GROUPS - 1)
            for g in (GROUPS - 2, GROUPS - 1):
                add_sums(STEPS - 1, g, STEPS - 1)
            close_slab(STEPS - 1)
            for k in range(3):
                layer_out(STEPS - 1, k)
            normalize(STEPS - 1)
            dve.wait_ge(acc_moved, 2 * STEPS)
            dve.wait_ge(layer_mm, 4 * (STEPS - 1) + 1)
            dve.tensor_copy(mslab[:, :], macc[:, 0:SLAB])
            dve.tensor_copy(dslab[:, :], dacc[:, 0:SLAB]).then_inc(slab_ready, 1)
            for k in range(3):
                layer_out(STEPS, k)
            normalize(STEPS)

            wrong = dve.value_load(flag[0:1, 0:1], min_val=0, max_val=NG * GROUP)
            with dve.If(wrong > 0):
                dve.memset(mfull[:, :], 0.0).then_inc(g_clear, 1)
                dve.memset(dfull[:, :], 0.0).then_inc(g_clear, 1)
                dve.wait_ge(g_clear, 2)
                def general_group(n):
                    wait(dve, g_mm, n * (TILES * NCH))
                    dve.tensor_copy(gdst[:, :], dst_f[:, bass.ds(n * TILES, TILES)]).then_inc(g_dst, 1)
                    dve.wait_ge(g_dst, n + 1)
                    for j in range(TILES):
                        m = n * TILES + j
                        dve.wait_ge(g_pre, m + 1)
                        dve.tensor_tensor(gpre[:, :], ps_h[:, 0, 0:P], c_rows[:, :], ALU.add).then_inc(g_added, 1)
                        dve.wait_ge(g_added, m + 1)
                        wait(dve, g_mm, m * NCH)
                        dve.scalar_tensor_tensor(out=h_sb[:, 0, 0:P], in0=gpre[:, :], scalar=SLOPE, in1=gpre[:, :],
                                                 op0=ALU.mult, op1=ALU.max).then_inc(g_h, 1)
                        for c in range(NCH):
                            k = m * NCH + c
                            wait(dve, g_mm, k)
                            dve.tensor_scalar(goh[:, :], iota_f[:, :], float(CHUNK * c), gdst[:, j:j + 1],
                                              ALU.add, ALU.is_equal).then_inc(g_oh, 1)
                            dve.wait_ge(g_mm, k + 1)
                            wait(dve, g_acc, k)
                            s = slice(c * CHUNK, (c + 1) * CHUNK)
                            dve.tensor_tensor(mfull[:, s], mfull[:, s], ps_x[:, 1, :], ALU.add)
                            dve.tensor_tensor(dfull[:, s], dfull[:, s], ps_h[0:1, 1, :], ALU.add).then_inc(g_acc, 1)

                general_group(0)
                with dve.Fori(1, NG) as n:
                    general_group(n)
                dve.wait_ge(g_acc, NG * TILES * NCH)
                with dve.Fori(0, SLABS) as s:
                    dve.wait_ge(layer_mm, (s + SLABS) * 4)
                    dve.tensor_copy(mslab[:, :], mfull[:, bass.ds(s * SLAB, SLAB)])
                    dve.tensor_copy(dslab[:, :], dfull[:, bass.ds(s * SLAB, SLAB)]).then_inc(slab_ready, 1)
                    for k in range(3):
                        layer_out(s + SLABS, k)
                    normalize(s + SLABS)


def kernel(**inputs):
    import numpy as np
    import concourse.bacc as bacc
    from concourse.bass_utils import run_bass_kernel_spmd as run

    a = {k.replace("L0_gnn_", ""): np.ascontiguousarray(v) for k, v in inputs.items()}
    padded = NG * GROUP

    def edges(v, fill):
        full = np.full((padded,) + v.shape[1:], fill, v.dtype)
        full[:EDGES] = v
        return full.reshape((NG, P, TILES) + v.shape[1:])

    xT = np.zeros((P, COLS), a["x"].dtype)
    xT[:, LEFT:LEFT + NODES] = a["x"].T
    a["WsT"], a["WdT"], a["T2T"] = a["Ws"].T, a["Wd"].T, a["T2"].T
    arrays = {
        "x": a["x"],
        "xT": xT,
        "srcT": edges(a["src"], 0).transpose(1, 0, 2).reshape(P, -1),
        "dstT": edges(a["dst"], NODES).transpose(1, 0, 2).reshape(P, -1),
        "eT": edges(a["edge_attr_32"], 0).transpose(0, 3, 2, 1).reshape(NG, EDIM, GROUP),
        "weights": np.stack([a[k] for k in W_NAMES], axis=1),
        "WeT": a["We"].T,
        "bcols": np.stack([a[k] for k in B_NAMES], axis=1),
        "brows": np.stack([a["tb1"], a["pb3"]])[None],
    }
    nc = bacc.Bacc("TRN2", target_bir_lowering=False, num_devices=1)
    feed, args = {}, []
    for name, v in arrays.items():
        feed[f"in_{name}"] = np.ascontiguousarray(v)
        args.append(nc.dram_tensor(f"in_{name}", v.shape, mybir.dt.from_np(v.dtype), kind="ExternalInput").ap())
    args.append(nc.dram_tensor("out_rows", (COLS, P), F32, kind="ExternalOutput").ap())
    gnn_resnorm(nc, *args)
    r = run(nc, [feed], core_ids=[0])
    return r.results[0]["out_rows"][LEFT:LEFT + NODES]
```

```python
from contextlib import ExitStack

import concourse.bass as bass
from concourse import mybir

F32 = mybir.dt.float32
BF16 = mybir.dt.bfloat16
I32 = mybir.dt.int32
ALU = mybir.AluOpType
ACT = mybir.ActivationFunctionType
AX = mybir.AxisListType

P = 128
NODES, EDGES, EDIM = 3125, 53125, 32
TILES = 4
GROUPS = 4
GROUP = TILES * P
STEPS = -(-EDGES // (GROUPS * GROUP))
NG = STEPS * GROUPS
SHIFT = 30
WIN = 96
SLAB = GROUPS * SHIFT
SPAN = SLAB - SHIFT + WIN
LEFT = NG // 2 * SHIFT + WIN // 2 - (NG + 1) * GROUP * NODES // (2 * EDGES)
SLABS = STEPS + 1
SLOPE = 0.2
EPS = 1e-5
CHUNK = 512
PEEL = 3
TBANKS = -(-NODES // 512)
TROWS = TBANKS * 4 * P
COLS = max(SLABS * SLAB, LEFT + TROWS)
NCH = -(-SLABS * SLAB // CHUNK)

assert NODES + LEFT < SHIFT * (NG - 1) + WIN and NODES + LEFT < COLS

W_NAMES = ["WsT", "T1", "WdT", "T2T", "Wpe", "Wpd", "P1", "P2", "P3"]
W_FIRST = 2
B_NAMES = ["be", "bs", "bd", "tb2", "bpd", "bpe", "pb1", "pb2"]


def gnn_resnorm(nc, xT, srcT, dstT, dstN, eT, weights, WeT, bcols, brows, out):
    with ExitStack() as ctx:
        def sb(name, shape, dt=F32):
            return ctx.enter_context(nc.sbuf_tensor(name, shape, dt))

        def psum(name, shape):
            return ctx.enter_context(nc.psum_tensor(name, shape, F32))

        def sem(name):
            return ctx.enter_context(nc.semaphore(name))

        table_src = nc.dram_tensor("table_src", (TROWS, P), F32, kind="Internal").ap()
        table_dst = nc.dram_tensor("table_dst", (LEFT + TROWS, P), F32, kind="Internal").ap()
        rel_rows = nc.dram_tensor("rel_rows", (NG, GROUP), BF16, kind="Internal").ap()

        w_sb = sb("w_sb", [P, len(W_NAMES), P])
        wet_sb = sb("wet_sb", [P, EDIM])
        bc_sb = sb("bc_sb", [P, len(B_NAMES)])
        br_sb = sb("br_sb", [1, 2, P])
        xt_sb = sb("xt_sb", [P, TROWS])
        tab_src = sb("tab_src", [P, TBANKS, 4, P])
        tab_dst = sb("tab_dst", [P, TBANKS, 4, P])
        zeros = sb("zeros", [LEFT, P])
        dst_i = sb("dst_i", [P, NG * TILES], I32)
        dst_f = sb("dst_f", [P, NG * TILES])
        rel = sb("rel", [P, NG, TILES])
        base_f = sb("base_f", [P, NG, TILES])
        bad = sb("bad", [P, NG * TILES])
        badsum = sb("badsum", [P, 1])
        flag = sb("flag", [1, 1], I32)
        reln_i = sb("reln_i", [NG, GROUP], I32)
        reln_f = sb("reln_f", [NG, GROUP])
        reln = sb("reln", [NG, GROUP], BF16)
        base_n = sb("base_n", [P, 1])
        iota_p = sb("iota_p", [P, 1])
        iota_f = sb("iota_f", [P, CHUNK])
        ident = sb("ident", [P, P])
        ones = sb("ones", [P, P])
        bsum = sb("bsum", [P, 2])
        hbias = sb("hbias", [P, 1])
        eps_sb = sb("eps_sb", [P, 1])
        w_src = sb("w_src", [P, P])
        w_dst = sb("w_dst", [P, P])
        w_msg = sb("w_msg", [P, P])
        c_rows = sb("c_rows", [P, P])
        deg_w = sb("deg_w", [P, P])

        idx = sb("idx", [P, 2, 2 * TILES], I32)
        xg = sb("xg", [P, GROUPS, GROUP])
        relb = sb("relb", [WIN, GROUPS, GROUP], BF16)
        oh = sb("oh", [P, GROUPS, TILES, WIN])
        ohsum = sb("ohsum", [P, GROUPS, WIN])
        lhs = sb("lhs", [P, GROUPS, GROUP])
        rhs = sb("rhs", [P, GROUPS, P])
        h_pre = sb("h_pre", [P, GROUP])
        h_sb = sb("h_sb", [P, 2, GROUP])
        acc = sb("acc", [P, 2, SPAN])
        slab = sb("slab", [P, 2, SLAB])
        xslab = sb("xslab", [P, SLAB])
        hid_in = sb("hid_in", [P, 3, SLAB])
        hid = sb("hid", [P, 3, SLAB])
        stats = sb("stats", [SLAB, 6])
        mv = sb("mv", [SLAB, 2])
        sd = sb("sd", [SLAB, 1])
        rstd = sb("rstd", [SLAB, 1])
        y_raw = sb("y_raw", [SLAB, P])
        y_sb = sb("y_sb", [SLAB, P])

        gsrc = sb("gsrc", [P, TILES], I32)
        gdst_i = sb("gdst_i", [P, TILES], I32)
        gdst = sb("gdst", [P, TILES])
        gpre = sb("gpre", [P, 2, P])
        goh = sb("goh", [P, CHUNK])
        full = sb("full", [P, 2, NCH * CHUNK])

        ps_t = psum("ps_t", [P, 4, GROUP])
        ps_h = psum("ps_h", [P, 2, GROUP])
        ps_m = psum("ps_m", [P, GROUP])
        ps_l = psum("ps_l", [P, GROUP])

        wfirst_in, wrest_in, b_in, dst_in, dstn_in = (sem(k) for k in ("wfirst_in", "wrest_in", "b_in", "dst_in", "dstn_in"))
        xt_in = [sem(f"xt_in{k}") for k in range((TBANKS + 1) // 2)]
        iota_done, ident_zero, ident_done = sem("iota_done"), sem("ident_zero"), sem("ident_done")
        ones_done, bias_sum, bias_done, acc_clear = sem("ones_done"), sem("bias_sum"), sem("bias_done"), sem("acc_clear")
        wsrc_mm, wsrc_copied, w_mm, w_copied = sem("wsrc_mm"), sem("wsrc_copied"), sem("w_mm"), sem("w_copied")
        ts_mm, ts_copied, ts_stored = sem("ts_mm"), sem("ts_copied"), sem("ts_stored")
        td_mm, td_copied, td_stored = sem("td_mm"), sem("td_copied"), sem("td_stored")
        rel_step, bad_done, flag_mm, flag_done = sem("rel_step"), sem("bad_done"), sem("flag_mm"), sem("flag_done")
        reln_step, reln_done, reln_stored = sem("reln_step"), sem("reln_done"), sem("reln_stored")
        idx_in = [sem(f"idx_in{h}") for h in range(2)]
        gathered = [sem(f"gathered{g}") for g in range(GROUPS)]
        e_in = [sem(f"e_in{g}") for g in range(GROUPS)]
        rows_in = [sem(f"rows_in{g}") for g in range(GROUPS)]
        relb_in = [sem(f"relb_in{g}") for g in range(GROUPS)]
        xslab_in = sem("xslab_in")
        oht_ready, oh_ready, ohsum_ready = sem("oht_ready"), sem("oh_ready"), sem("ohsum_ready")
        pre_done, pre_added, h_ready = sem("pre_done"), sem("pre_added"), sem("h_ready")
        seg_done, acc_added = sem("seg_done"), sem("acc_added")
        acc_moved, slab_ready = sem("acc_moved"), sem("slab_ready")
        layer_mm, layer_biased, layer_act = sem("layer_mm"), sem("layer_biased"), sem("layer_act")
        stats_done, var_done, sd_done, rstd_done = sem("stats_done"), sem("var_done"), sem("sd_done"), sem("rstd_done")
        y_ready, y_out = sem("y_ready"), sem("y_out")
        g_in, g_dst, g_gath, g_pre = sem("g_in"), sem("g_dst"), sem("g_gath"), sem("g_pre")
        g_added, g_h, g_oh, g_mm, g_acc, g_clear = (sem(k) for k in ("g_added", "g_h", "g_oh", "g_mm", "g_acc", "g_clear"))

        def W(name):
            return w_sb[:, W_NAMES.index(name), :]

        def B(name, n=1):
            k = B_NAMES.index(name)
            return bc_sb[:, k:k + n]

        def wait(eng, s, value):
            if not isinstance(value, int) or value > 0:
                eng.wait_ge(s, value)

        def bank_rows(table, b, first):
            return table[first + b * 4 * P:first + (b + 1) * 4 * P, :].rearrange("(c p) f -> p c f", p=P)

        block = ctx.enter_context(nc.Block())

        @block.sync
        def _(sp):
            def load_idx(i, half):
                for g in (2 * half, 2 * half + 1):
                    wait(sp, gathered[g], 16 * TILES * i)
                c = (i * (GROUPS * TILES)) + half * 2 * TILES
                sp.dma_start(idx[:, half, :], srcT[:, bass.ds(c, 2 * TILES)]).then_inc(idx_in[half], 16)

            def load_xslab(s, col):
                wait(sp, layer_mm, s * 4)
                sp.dma_start(xslab[:, :], xT[:, bass.ds(col, SLAB)]).then_inc(xslab_in, 16)

            def load_group(i, g):
                n = i * GROUPS + g
                wait(sp, pre_done, n - GROUPS + 1)
                sp.dma_start(relb[:, g, :], rel_rows[bass.ds(n, 1), :].to_broadcast([WIN, GROUP])).then_inc(relb_in[g], 16)
                sp.dma_start(lhs[WIN:P, g, :], eT[n]).then_inc(e_in[g], 16)
                sp.dma_start(rhs[0:WIN, g, :], table_dst[bass.ds(i * SLAB + g * SHIFT, WIN), :]).then_inc(rows_in[g], 16)

            def step(i, k, last):
                load_group(i, 0)
                load_idx(i, 1)
                load_group(i, 1)
                if k >= 1:
                    load_xslab(i - 1, (i - 1) * SLAB)
                load_group(i, 2)
                if not last:
                    load_idx(i + 1, 0)
                load_group(i, 3)

            sp.dma_start(w_sb[:, 0:W_FIRST, :], weights[:, 0:W_FIRST, :]).then_inc(wfirst_in, 16)
            for k in range(len(xt_in)):
                c = slice(k * 8 * P, min((k + 1) * 8 * P, TROWS))
                sp.dma_start(xt_sb[:, c], xT[:, LEFT + c.start:LEFT + c.stop]).then_inc(xt_in[k], 16)
            sp.dma_start(w_sb[:, W_FIRST:, :], weights[:, W_FIRST:, :]).then_inc(wrest_in, 16)
            load_idx(0, 0)
            for b in range(TBANKS):
                sp.wait_ge(ts_copied, b + 1)
                sp.dma_start(bank_rows(table_src, b, 0), tab_src[:, b, :, :]).then_inc(ts_stored, 16)
            sp.wait_ge(reln_done, 1)
            sp.dma_start(rel_rows, reln[:, :]).then_inc(reln_stored, 16)
            sp.wait_ge(ones_done, 1)
            sp.dma_start(table_dst[0:LEFT, :], zeros[:, :]).then_inc(td_stored, 16)
            for b in range(TBANKS):
                sp.wait_ge(td_copied, b + 1)
                sp.dma_start(bank_rows(table_dst, b, LEFT), tab_dst[:, b, :, :]).then_inc(td_stored, 16)
            sp.wait_ge(reln_stored, 16)
            sp.wait_ge(td_stored, 16 * (TBANKS + 1))
            for i in range(PEEL):
                step(i, i, False)
            with sp.Fori(PEEL, STEPS - 1) as i:
                step(i, PEEL, False)
            step(STEPS - 1, PEEL, True)
            for s in range(STEPS - 1, SLABS):
                load_xslab(s, s * SLAB)

            sp.wait_ge(flag_done, 1)
            wrong = sp.value_load(flag[0:1, 0:1], min_val=0, max_val=NG * GROUP)
            with sp.If(wrong > 0):
                def general_group(n):
                    wait(sp, g_mm, n * (TILES * NCH))
                    sp.dma_start(gsrc[:, :], srcT[:, bass.ds(n * TILES, TILES)]).then_inc(g_in, 16)
                    sp.dma_start(lhs[WIN:P, 0, :], eT[n]).then_inc(g_in, 16)

                general_group(0)
                with sp.Fori(1, NG) as n:
                    general_group(n)
                with sp.Fori(0, SLABS) as s:
                    load_xslab(s + SLABS, s * SLAB)

        @block.gpsimd
        def _(pool):
            bound, nothing = pool.alloc_register("bound"), pool.alloc_register("nothing")
            pool.reg_mov(nothing, 0)

            def gather(i, g):
                n = i * GROUPS + g
                wait(pool, pre_added, n - GROUPS + 1)
                if g % 2 == 0:
                    pool.wait_ge(idx_in[g // 2], (i + 1) * 16)
                pool.reg_add(bound, nothing, NODES - 1)
                for j in range(TILES):
                    col = (g % 2) * TILES + j
                    pool.indirect_dma_start(
                        out=xg[:, g, j * P:(j + 1) * P], out_offset=None, in_=table_src[:, :],
                        in_offset=bass.IndirectOffsetOnAxis(ap=idx[:, g // 2, col:col + 1], axis=0),
                        bounds_check=bound, oob_is_err=True).then_inc(gathered[g], 16)

            pool.iota(iota_p[:, :], [[0, 1]], base=0, channel_multiplier=1,
                      allow_small_or_imprecise_dtypes=True).then_inc(iota_done, 1)
            pool.iota(base_n[:, :], [[0, 1]], base=LEFT, channel_multiplier=-SHIFT,
                      allow_small_or_imprecise_dtypes=True).then_inc(iota_done, 1)
            pool.iota(iota_f[:, :], [[1, CHUNK]], base=0, channel_multiplier=0,
                      allow_small_or_imprecise_dtypes=True).then_inc(iota_done, 1)
            pool.iota(base_f[:, :, :], [[SHIFT, NG], [0, TILES]], base=0, channel_multiplier=0,
                      allow_small_or_imprecise_dtypes=True).then_inc(iota_done, 1)
            pool.memset(ident[:, :], 0.0).then_inc(ident_zero, 1)
            pool.wait_ge(ident_zero, 1)
            pool.affine_select(out=ident[:, :], in_=ident[:, :], compare_op=ALU.not_equal, fill=1.0,
                               base=0, pattern=[[-1, P]], channel_multiplier=1).then_inc(ident_done, 1)
            pool.wait_ge(ts_stored, 16 * TBANKS)
            for i in range(PEEL):
                for g in range(GROUPS):
                    gather(i, g)
            with pool.Fori(PEEL, STEPS) as i:
                for g in range(GROUPS):
                    gather(i, g)

            pool.wait_ge(flag_done, 1)
            wrong = pool.value_load(flag[0:1, 0:1], min_val=0, max_val=NG * GROUP)
            with pool.If(wrong > 0):
                def general_gathers(n):
                    pool.wait_ge(g_in, (n + 1) * 32)
                    pool.wait_ge(g_dst, (n + 1) * 2)
                    wait(pool, g_h, n * TILES)
                    pool.reg_add(bound, nothing, TROWS - 1)
                    for side, table, index in ((0, table_src, gsrc), (1, table_dst, gdst_i)):
                        for j in range(TILES):
                            pool.indirect_dma_start(
                                out=xg[:, side, j * P:(j + 1) * P], out_offset=None, in_=table[:, :],
                                in_offset=bass.IndirectOffsetOnAxis(ap=index[:, j:j + 1], axis=0),
                                bounds_check=bound, oob_is_err=True).then_inc(g_gath, 16)

                general_gathers(0)
                with pool.Fori(1, NG) as n:
                    general_gathers(n)

        @block.tensor
        def _(pe):
            pe.wait_ge(wfirst_in, 16)
            pe.matmul(ps_m[:, 0:P], W("WsT"), W("T1"), start=True, stop=True).then_inc(wsrc_mm, 1)
            pe.wait_ge(wsrc_copied, 1)
            for b in range(TBANKS):
                pe.wait_ge(xt_in[b // 2], 16)
                wait(pe, ts_copied, b - 1)
                for c in range(4):
                    k = (b * 4 + c) * P
                    mm = pe.matmul(ps_t[:, b % 2, c * P:(c + 1) * P], xt_sb[:, k:k + P], w_src[:, :], start=True, stop=True)
                mm.then_inc(ts_mm, 1)
            pe.wait_ge(wrest_in, 16)
            pe.wait_ge(b_in, 48)
            pe.wait_ge(bias_done, 1)
            pe.wait_ge(ones_done, 1)
            pe.matmul(ps_h[:, 0, 0:P], W("WdT"), W("T1"), start=True, stop=True)
            pe.matmul(ps_h[:, 0, P:2 * P], W("T2T"), W("Wpe"), start=True, stop=True)
            pe.matmul(ps_h[:, 0, 2 * P:3 * P], bsum[:, 1:2].to_broadcast([P, P]), W("T1"), start=True, stop=False)
            pe.matmul(ps_h[:, 0, 2 * P:3 * P], ones[0:1, :], br_sb[0:1, 0, :], start=False, stop=True)
            pe.matmul(ps_h[:, 0, 3 * P:], B("tb2").to_broadcast([P, P]), W("Wpe"), start=True, stop=True)
            pe.matmul(ps_h[WIN:P, 1, 0:P], wet_sb[:, :], W("T1"), start=True, stop=True).then_inc(w_mm, 1)
            pe.wait_ge(w_copied, 1)
            for b in range(TBANKS):
                wait(pe, td_copied, b - 1)
                for c in range(4):
                    k = (b * 4 + c) * P
                    mm = pe.matmul(ps_t[:, 2 + b % 2, c * P:(c + 1) * P], xt_sb[:, k:k + P], w_dst[:, :], start=True, stop=True)
                mm.then_inc(td_mm, 1)
            pe.wait_ge(bad_done, 1)
            pe.matmul(ps_m[0:1, 0:1], badsum[:, :], ones[:, 0:1], start=True, stop=True).then_inc(flag_mm, 1)
            pe.wait_ge(flag_done, 1)
            pe.wait_ge(ident_done, 1)

            def pre(i, g):
                n = i * GROUPS + g
                pe.wait_ge(oht_ready, n + 1)
                pe.wait_ge(rows_in[g], (i + 1) * 16)
                pe.wait_ge(e_in[g], (i + 1) * 16)
                wait(pe, pre_added, n - 1)
                for j in range(TILES):
                    c = slice(j * P, (j + 1) * P)
                    mm = pe.matmul(ps_h[:, g % 2, c], lhs[:, g, c], rhs[:, g, :], start=True, stop=True)
                mm.then_inc(pre_done, 1)

            def seg(i, g):
                n = i * GROUPS + g
                pe.wait_ge(oh_ready, n + 1)
                wait(pe, acc_added, n)
                pe.wait_ge(h_ready, n + 1)
                for j in range(TILES):
                    mm = pe.matmul(ps_m[:, 0:WIN], h_sb[:, g % 2, j * P:(j + 1) * P], oh[:, g, j, :],
                                   start=(j == 0), stop=(j == TILES - 1))
                mm.then_inc(seg_done, 1)

            def layer(s, k):
                o = ps_l[:, 0:SLAB]
                if k == 0:
                    wait(pe, y_ready, s)
                    pe.wait_ge(xslab_in, s * 16 + 16)
                    pe.wait_ge(slab_ready, s + 1)
                    pe.matmul(o, W("Wpd"), xslab[:, :], start=True, stop=False)
                    pe.matmul(o, deg_w[:, :], slab[:, 1, :], start=False, stop=False)
                    pe.matmul(o, w_msg[:, :], slab[:, 0, :], start=False, stop=True).then_inc(layer_mm, 1)
                elif k < 3:
                    pe.wait_ge(layer_act, s * 3 + k)
                    pe.matmul(o, W(f"P{k}"), hid[:, k - 1, :], start=True, stop=True).then_inc(layer_mm, 1)
                else:
                    pe.wait_ge(layer_act, s * 3 + 3)
                    o = ps_l[0:SLAB, 0:P]
                    pe.matmul(o, hid[:, 2, :], W("P3"), start=True, stop=False)
                    pe.matmul(o, ones[0:1, 0:SLAB], br_sb[0:1, 1, :], start=False, stop=False)
                    pe.matmul(o, xslab[:, :], ident[:, :], start=False, stop=True).then_inc(layer_mm, 1)

            def step(i, k):
                for g in range(GROUPS):
                    pre(i, g)
                    if g >= 2 and k >= 1:
                        layer(i - 1, 2 * (g - 2))
                    if g >= 1:
                        seg(i, g - 1)
                    elif k >= 1:
                        seg(i - 1, GROUPS - 1)
                    if g >= 2 and k >= 1:
                        layer(i - 1, 2 * (g - 2) + 1)

            for i in range(PEEL):
                step(i, i)
            with pe.Fori(PEEL, STEPS) as i:
                step(i, PEEL)
            seg(STEPS - 1, GROUPS - 1)
            for s in range(STEPS - 1, SLABS):
                for k in range(4):
                    layer(s, k)

            wrong = pe.value_load(flag[0:1, 0:1], min_val=0, max_val=NG * GROUP)
            with pe.If(wrong > 0):
                def general_group(n):
                    pe.wait_ge(g_in, (n + 1) * 32)
                    for j in range(TILES):
                        m = n * TILES + j
                        wait(pe, g_h, m)
                        pe.matmul(ps_h[:, 0, 0:P], lhs[WIN:P, 0, j * P:(j + 1) * P], rhs[WIN:P, 0, :],
                                  start=True, stop=True).then_inc(g_pre, 1)
                        pe.wait_ge(g_h, m + 1)
                        for c in range(NCH):
                            q = m * NCH + c
                            wait(pe, g_acc, q)
                            pe.wait_ge(g_oh, q + 1)
                            pe.matmul(ps_t[:, 0, :], h_sb[:, 0, 0:P], goh[:, :], start=True, stop=True).then_inc(g_mm, 1)

                general_group(0)
                with pe.Fori(1, NG) as n:
                    general_group(n)
                with pe.Fori(0, SLABS) as s:
                    for k in range(4):
                        layer(s + SLABS, k)

        @block.scalar
        def _(act):
            act.dma_start(bc_sb[:, :], bcols).then_inc(b_in, 16)
            act.dma_start(br_sb[:, :, :], brows).then_inc(b_in, 16)
            act.dma_start(wet_sb[:, :], WeT).then_inc(b_in, 16)
            act.dma_start(reln_i[:, :], dstN).then_inc(dstn_in, 16)
            act.dma_start(dst_i[:, :], dstT).then_inc(dst_in, 16)
            for b in range(TBANKS):
                act.wait_ge(ts_mm, b + 1)
                act.activation(tab_src[:, b, :, :].rearrange("p c f -> p (c f)"), ps_t[:, b % 2, :], ACT.Copy).then_inc(ts_copied, 1)

            def layer_out(s, k):
                act.wait_ge(layer_mm, s * 4 + (k + 1))
                b = [hbias[:, :], B("pb1"), B("pb2")][k]
                act.activation(hid_in[:, k, :], ps_l[:, 0:SLAB], ACT.Identity, bias=b).then_inc(layer_biased, 1)

            def deviation(s):
                act.wait_ge(var_done, s + 1)
                act.activation(sd[:, :], mv[:, 1:2], ACT.Sqrt, bias=eps_sb[0:SLAB, :]).then_inc(sd_done, 1)

            def store(s, before=0):
                act.wait_ge(y_ready, s + (before + 1))
                act.dma_start(out[bass.ds(s * SLAB, SLAB), :], y_sb[:, :]).then_inc(y_out, 16)

            def step(i, k):
                if k >= 2:
                    deviation(i - 2)
                    store(i - 2)
                if k >= 1:
                    for layer in range(3):
                        layer_out(i - 1, layer)

            act.wait_ge(bias_done, 2)
            for i in range(PEEL):
                step(i, i)
            with act.Fori(PEEL, STEPS) as i:
                step(i, PEEL)
            deviation(STEPS - 2)
            store(STEPS - 2)
            for s in range(STEPS - 1, SLABS):
                for k in range(3):
                    layer_out(s, k)
                deviation(s)
                store(s)
            act.wait_ge(y_out, 16 * SLABS)

            act.wait_ge(flag_done, 1)
            wrong = act.value_load(flag[0:1, 0:1], min_val=0, max_val=NG * GROUP)
            with act.If(wrong > 0):
                with act.Fori(0, SLABS) as s:
                    for k in range(3):
                        layer_out(s + SLABS, k)
                    deviation(s + SLABS)
                    store(s, SLABS)
                act.wait_ge(y_out, 32 * SLABS)

        @block.vector
        def _(dve):
            dve.memset(zeros[:, :], 0.0)
            dve.memset(ones[:, :], 1.0).then_inc(ones_done, 1)
            dve.memset(eps_sb[:, :], EPS)
            dve.memset(acc[:, :, :], 0.0).then_inc(acc_clear, 1)
            dve.wait_ge(b_in, 48)
            dve.tensor_tensor(bsum[:, 0:1], B("be"), B("bs"), ALU.add).then_inc(bias_sum, 1)
            dve.wait_ge(bias_sum, 1)
            dve.tensor_tensor(bsum[:, 1:2], bsum[:, 0:1], B("bd"), ALU.add).then_inc(bias_done, 1)
            dve.tensor_tensor(hbias[:, :], B("bpd"), B("bpe"), ALU.add).then_inc(bias_done, 1)
            dve.wait_ge(wsrc_mm, 1)
            dve.tensor_copy(w_src[:, :], ps_m[:, 0:P]).then_inc(wsrc_copied, 1)
            dve.wait_ge(iota_done, 4)
            dve.wait_ge(dstn_in, 16)
            dve.tensor_scalar(reln_f[:, :], reln_i[:, :], base_n[0:NG, :], -1.0, ALU.add, ALU.max).then_inc(reln_step, 1)
            dve.wait_ge(reln_step, 1)
            dve.tensor_scalar(reln[:, :], reln_f[:, :], float(WIN), None, ALU.min).then_inc(reln_done, 1)
            dve.wait_ge(dst_in, 16)
            dve.tensor_scalar(dst_f[:, :], dst_i[:, :], float(LEFT), None, ALU.add).then_inc(rel_step, 1)
            dve.wait_ge(rel_step, 1)
            relv = rel[:, :, :].rearrange("p n j -> p (n j)")
            dve.tensor_tensor(relv, dst_f[:, :], base_f[:, :, :].rearrange("p n j -> p (n j)"),
                              ALU.subtract).then_inc(rel_step, 1)
            dve.wait_ge(rel_step, 2)
            dve.tensor_scalar(bad[:, :], relv, 0.0, None, ALU.is_lt).then_inc(rel_step, 1)
            dve.wait_ge(rel_step, 3)
            dve.scalar_tensor_tensor(out=bad[:, :], in0=relv, scalar=float(WIN - 1), in1=bad[:, :],
                                     op0=ALU.is_gt, op1=ALU.add).then_inc(rel_step, 1)
            dve.wait_ge(rel_step, 4)
            dve.tensor_reduce(badsum[:, :], bad[:, :], AX.X, ALU.add).then_inc(bad_done, 1)
            dve.wait_ge(w_mm, 1)
            dve.tensor_copy(w_msg[:, :], ps_h[:, 0, P:2 * P])
            dve.tensor_copy(deg_w[:, :], ps_h[:, 0, 3 * P:])
            for g in range(GROUPS):
                dve.tensor_copy(rhs[WIN:P, g, :], ps_h[WIN:P, 1, 0:P])
            dve.tensor_copy(c_rows[:, :], ps_h[:, 0, 2 * P:3 * P])
            dve.tensor_copy(w_dst[:, :], ps_h[:, 0, 0:P]).then_inc(w_copied, 1)
            dve.wait_ge(w_copied, 1)
            for b in range(TBANKS):
                dve.wait_ge(td_mm, b + 1)
                dve.tensor_tensor(tab_dst[:, b, :, :], ps_t[:, 2 + b % 2, :].rearrange("p (c f) -> p c f", c=4),
                                  c_rows[:, None, :].to_broadcast([P, 4, P]), ALU.add).then_inc(td_copied, 1)
            dve.wait_ge(flag_mm, 1)
            dve.tensor_copy(flag[:, :], ps_m[0:1, 0:1]).then_inc(flag_done, 1)
            dve.wait_ge(acc_clear, 1)

            def one_hots(i, g):
                n = i * GROUPS + g
                dve.wait_ge(relb_in[g], (i + 1) * 16)
                wait(dve, pre_done, n - GROUPS + 1)
                dve.tensor_scalar(lhs[0:WIN, g, :], relb[:, g, :], iota_p[0:WIN, :], None, ALU.is_equal).then_inc(oht_ready, 1)
                wait(dve, seg_done, n - GROUPS + 1)
                dve.tensor_tensor(
                    oh[:, g, :, :], iota_f[:, None, 0:WIN].to_broadcast([P, TILES, WIN]),
                    rel[:, bass.ds(n, 1), :].rearrange("p a j -> p (a j)")[:, :, None].to_broadcast([P, TILES, WIN]),
                    ALU.is_equal).then_inc(oh_ready, 1)
                dve.wait_ge(oh_ready, n + 1)
                dve.tensor_reduce(ohsum[:, g, :], oh[:, g, :, :].rearrange("p j w -> p w j"), AX.X,
                                  ALU.add).then_inc(ohsum_ready, 1)

            def hidden(i, g):
                n = i * GROUPS + g
                dve.wait_ge(pre_done, n + 1)
                dve.wait_ge(gathered[g], (i + 1) * (16 * TILES))
                wait(dve, h_ready, n)
                dve.tensor_tensor(h_pre[:, :], ps_h[:, g % 2, :], xg[:, g, :], ALU.add).then_inc(pre_added, 1)
                dve.wait_ge(pre_added, n + 1)
                wait(dve, seg_done, n - 1)
                dve.scalar_tensor_tensor(out=h_sb[:, g % 2, :], in0=h_pre[:, :], scalar=SLOPE, in1=h_pre[:, :],
                                         op0=ALU.mult, op1=ALU.max).then_inc(h_ready, 1)

            def layer_out(s, k):
                dve.wait_ge(layer_biased, s * 3 + (k + 1))
                dve.scalar_tensor_tensor(out=hid[:, k, :], in0=hid_in[:, k, :], scalar=SLOPE, in1=hid_in[:, k, :],
                                         op0=ALU.mult, op1=ALU.max).then_inc(layer_act, 1)

            def add_sums(i, g, moves):
                n = i * GROUPS + g
                wait(dve, acc_moved, moves * 2)
                wait(dve, acc_added, n)
                dve.wait_ge(ohsum_ready, n + 1)
                o = g * SHIFT
                dve.tensor_tensor(acc[:, 1, o:o + WIN], acc[:, 1, o:o + WIN], ohsum[:, g, :], ALU.add)
                dve.wait_ge(seg_done, n + 1)
                dve.tensor_tensor(acc[:, 0, o:o + WIN], acc[:, 0, o:o + WIN], ps_m[:, 0:WIN], ALU.add).then_inc(acc_added, 1)

            def close_slab(s):
                dve.wait_ge(acc_added, (s + 1) * GROUPS)
                wait(dve, layer_mm, s * 4)
                dve.tensor_copy(slab[:, :, :], acc[:, :, 0:SLAB]).then_inc(slab_ready, 1)
                dve.wait_ge(slab_ready, s + 1)
                dve.tensor_copy(acc[:, :, 0:SPAN - SLAB], acc[:, :, SLAB:SPAN]).then_inc(acc_moved, 1)
                dve.wait_ge(acc_moved, s * 2 + 1)
                dve.memset(acc[:, :, SPAN - SLAB:SPAN], 0.0).then_inc(acc_moved, 1)

            def statistics(s):
                y = ps_l[0:SLAB, 0:P]
                dve.wait_ge(layer_mm, s * 4 + 4)
                dve.bn_stats(stats[:, :], y).then_inc(stats_done, 1)
                dve.wait_ge(stats_done, s + 1)
                dve.tensor_copy(y_raw[:, :], y)
                dve.bn_aggr(mv[:, :], stats[:, :]).then_inc(var_done, 1)

            def normalize(s):
                dve.wait_ge(sd_done, s + 1)
                dve.reciprocal(rstd[:, :], sd[:, :]).then_inc(rstd_done, 1)
                wait(dve, y_out, s * 16)
                dve.wait_ge(rstd_done, s + 1)
                dve.tensor_scalar(y_sb[:, :], y_raw[:, :], mv[:, 0:1], rstd[:, 0:1], ALU.subtract,
                                  ALU.mult).then_inc(y_ready, 1)

            def step(i, k):
                for g in range(GROUPS):
                    one_hots(i, g)
                    if g == 0 and k >= 2:
                        statistics(i - 2)
                    if g >= 1:
                        hidden(i, g - 1)
                    elif k >= 1:
                        hidden(i - 1, GROUPS - 1)
                    if g == 0 and k >= 2:
                        normalize(i - 2)
                    if g >= 2 and k >= 1:
                        layer_out(i - 1, 2 * (g - 2))
                    if g >= 2:
                        add_sums(i, g - 2, i)
                    elif k >= 1:
                        add_sums(i - 1, g + GROUPS - 2, i - 1)
                    if g == 2 and k >= 1:
                        layer_out(i - 1, 1)
                    if g == 1 and k >= 1:
                        close_slab(i - 1)

            for i in range(PEEL):
                step(i, i)
            with dve.Fori(PEEL, STEPS) as i:
                step(i, PEEL)
            statistics(STEPS - 2)
            hidden(STEPS - 1, GROUPS - 1)
            normalize(STEPS - 2)
            for g in (GROUPS - 2, GROUPS - 1):
                add_sums(STEPS - 1, g, STEPS - 1)
            close_slab(STEPS - 1)
            for k in range(3):
                layer_out(STEPS - 1, k)
            statistics(STEPS - 1)
            normalize(STEPS - 1)
            dve.wait_ge(acc_moved, 2 * STEPS)
            dve.tensor_copy(slab[:, :, :], acc[:, :, 0:SLAB]).then_inc(slab_ready, 1)
            for k in range(3):
                layer_out(STEPS, k)
            statistics(STEPS)
            normalize(STEPS)

            wrong = dve.value_load(flag[0:1, 0:1], min_val=0, max_val=NG * GROUP)
            with dve.If(wrong > 0):
                dve.memset(full[:, :, :], 0.0).then_inc(g_clear, 1)
                dve.wait_ge(g_clear, 1)

                def general_group(n):
                    wait(dve, g_mm, n * (TILES * NCH))
                    dve.tensor_copy(gdst[:, :], dst_f[:, bass.ds(n * TILES, TILES)]).then_inc(g_dst, 1)
                    dve.tensor_copy(gdst_i[:, :], dst_f[:, bass.ds(n * TILES, TILES)]).then_inc(g_dst, 1)
                    dve.wait_ge(g_dst, (n + 1) * 2)
                    dve.wait_ge(g_gath, (n + 1) * (32 * TILES))
                    for j in range(TILES):
                        m = n * TILES + j
                        c = slice(j * P, (j + 1) * P)
                        dve.wait_ge(g_pre, m + 1)
                        dve.tensor_tensor(gpre[:, 0, :], ps_h[:, 0, 0:P], xg[:, 0, c], ALU.add).then_inc(g_added, 1)
                        dve.wait_ge(g_added, m * 2 + 1)
                        dve.tensor_tensor(gpre[:, 1, :], gpre[:, 0, :], xg[:, 1, c], ALU.add).then_inc(g_added, 1)
                        wait(dve, g_mm, m * NCH)
                        dve.wait_ge(g_added, m * 2 + 2)
                        dve.scalar_tensor_tensor(out=h_sb[:, 0, 0:P], in0=gpre[:, 1, :], scalar=SLOPE, in1=gpre[:, 1, :],
                                                 op0=ALU.mult, op1=ALU.max).then_inc(g_h, 1)
                        for k in range(NCH):
                            q = m * NCH + k
                            wait(dve, g_mm, q)
                            wait(dve, g_acc, q)
                            dve.tensor_scalar(goh[:, :], iota_f[:, :], float(CHUNK * k), gdst[:, j:j + 1],
                                              ALU.add, ALU.is_equal).then_inc(g_oh, 1)
                            dve.wait_ge(g_oh, q + 1)
                            part = slice(k * CHUNK, (k + 1) * CHUNK)
                            dve.tensor_tensor(full[:, 1, part], full[:, 1, part], goh[:, :], ALU.add)
                            dve.wait_ge(g_mm, q + 1)
                            dve.tensor_tensor(full[:, 0, part], full[:, 0, part], ps_t[:, 0, :], ALU.add).then_inc(g_acc, 1)

                general_group(0)
                with dve.Fori(1, NG) as n:
                    general_group(n)
                dve.wait_ge(g_acc, NG * TILES * NCH)
                with dve.Fori(0, SLABS) as s:
                    dve.wait_ge(layer_mm, (s + SLABS) * 4)
                    dve.tensor_copy(slab[:, :, :], full[:, :, bass.ds(s * SLAB, SLAB)]).then_inc(slab_ready, 1)
                    for k in range(3):
                        layer_out(s + SLABS, k)
                    statistics(s + SLABS)
                    normalize(s + SLABS)


def kernel(**inputs):
    import numpy as np
    import concourse.bacc as bacc
    from concourse.bass_utils import run_bass_kernel_spmd as run

    a = {k.replace("L0_gnn_", ""): np.ascontiguousarray(v) for k, v in inputs.items()}
    padded = NG * GROUP

    def edges(v, fill):
        full = np.full((padded,) + v.shape[1:], fill, v.dtype)
        full[:EDGES] = v
        return full.reshape((NG, P, TILES) + v.shape[1:])

    xT = np.zeros((P, COLS), a["x"].dtype)
    xT[:, LEFT:LEFT + NODES] = a["x"].T
    a["WsT"], a["WdT"], a["T2T"] = a["Ws"].T, a["Wd"].T, a["T2"].T
    arrays = {
        "xT": xT,
        "srcT": edges(a["src"], 0).transpose(1, 0, 2).reshape(P, -1),
        "dstT": edges(a["dst"], NODES).transpose(1, 0, 2).reshape(P, -1),
        "dstN": edges(a["dst"], NODES).transpose(0, 2, 1).reshape(NG, GROUP),
        "eT": edges(a["edge_attr_32"], 0).transpose(0, 3, 2, 1).reshape(NG, EDIM, GROUP),
        "weights": np.stack([a[k] for k in W_NAMES], axis=1),
        "WeT": a["We"].T,
        "bcols": np.stack([a[k] for k in B_NAMES], axis=1),
        "brows": np.stack([a["tb1"], a["pb3"]])[None],
    }
    nc = bacc.Bacc("TRN2", target_bir_lowering=False, num_devices=1)
    feed, args = {}, []
    for name, v in arrays.items():
        feed[f"in_{name}"] = np.ascontiguousarray(v)
        args.append(nc.dram_tensor(f"in_{name}", v.shape, mybir.dt.from_np(v.dtype), kind="ExternalInput").ap())
    args.append(nc.dram_tensor("out_rows", (SLABS * SLAB, P), F32, kind="ExternalOutput").ap())
    gnn_resnorm(nc, *args)
    r = run(nc, [feed], core_ids=[0])
    return r.results[0]["out_rows"][LEFT:LEFT + NODES]
```

```python
from contextlib import ExitStack

import concourse.bass as bass
from concourse import mybir

F32 = mybir.dt.float32
I32 = mybir.dt.int32
ALU = mybir.AluOpType
ACT = mybir.ActivationFunctionType
AX = mybir.AxisListType

P = 128
NODES, EDGES, EDIM = 3125, 53125, 32
TILES = 4
GROUPS = 4
GROUP = TILES * P
STEPS = -(-EDGES // (GROUPS * GROUP))
NG = STEPS * GROUPS
SHIFT = 30
WIN = 96
SLAB = GROUPS * SHIFT
SPAN = SLAB - SHIFT + WIN
LEFT = NG // 2 * SHIFT + WIN // 2 - (NG + 1) * GROUP * NODES // (2 * EDGES)
SLABS = STEPS + 1
SLOPE = 0.2
EPS = 1e-5
CHUNK = 512
PEEL = 3
TCHUNKS = -(-NODES // P)
TBANKS = -(-TCHUNKS // 4)
TROWS = TCHUNKS * P
LAST = SHIFT * (NG - 1)
OUT_ROWS = LEFT + NODES
COLS = max(LAST + WIN, LEFT + TROWS)
END = SLAB - SHIFT
TAIL = OUT_ROWS - LAST
NCH = -(-(LAST + WIN) // CHUNK)

assert 0 < TAIL < WIN

W_NAMES = ["WsT", "T1", "WdT", "T2T", "Wpe", "Wpd", "P1", "P2", "P3"]
W_FIRST = 2
B_NAMES = ["be", "bs", "bd", "tb2", "bpd", "bpe", "pb1", "pb2"]


def gnn_resnorm(nc, x, xT, srcT, dstT, eT, weights, WeT, bcols, brows, out):
    with ExitStack() as ctx:
        def sb(name, shape, dt=F32):
            return ctx.enter_context(nc.sbuf_tensor(name, shape, dt))

        def psum(name, shape):
            return ctx.enter_context(nc.psum_tensor(name, shape, F32))

        def sem(name):
            return ctx.enter_context(nc.semaphore(name))

        table_src = nc.dram_tensor("table_src", (TROWS, P), F32, kind="Internal").ap()
        table_dst = nc.dram_tensor("table_dst", (TROWS, P), F32, kind="Internal").ap()

        w_sb = sb("w_sb", [P, len(W_NAMES), P])
        wet_sb = sb("wet_sb", [P, EDIM])
        bc_sb = sb("bc_sb", [P, len(B_NAMES)])
        br_sb = sb("br_sb", [1, 2, P])
        xt_sb = sb("xt_sb", [P, COLS])
        tab = sb("tab", [P, TCHUNKS, P])
        dst_i = sb("dst_i", [P, NG * TILES], I32)
        dst_f = sb("dst_f", [P, NG * TILES])
        rel = sb("rel", [P, NG, TILES])
        base_f = sb("base_f", [P, NG])
        bad = sb("bad", [P, NG * TILES])
        badsum = sb("badsum", [P, 1])
        flag = sb("flag", [1, 1], I32)
        iota_f = sb("iota_f", [P, WIN])
        ident = sb("ident", [P, P])
        ones = sb("ones", [P, P])
        bsum = sb("bsum", [P, 2])
        bias = sb("bias", [P, 2, 3])
        w_neg = sb("w_neg", [P, 3, P])
        eps_sb = sb("eps_sb", [P, 1])
        w_src = sb("w_src", [P, P])
        w_dst = sb("w_dst", [P, P])
        w_msg = sb("w_msg", [P, P])
        c_rows = sb("c_rows", [P, P])
        deg_w = sb("deg_w", [P, P])

        idx = sb("idx", [P, 2, 2 * TILES], I32)
        xg = sb("xg", [P, GROUPS, GROUP])
        xgt = sb("xgt", [P, 2, GROUP])
        xspan = sb("xspan", [P, SPAN])
        oh = sb("oh", [P, GROUPS, TILES, WIN])
        ohsum = sb("ohsum", [P, GROUPS, WIN])
        lhs = sb("lhs", [P, GROUPS, GROUP])
        rhs = sb("rhs", [P, GROUPS, P])
        h_pre = sb("h_pre", [P, GROUP])
        h_sb = sb("h_sb", [P, 2, GROUP])
        acc = sb("acc", [P, 2, SPAN])
        slab = sb("slab", [P, 2, SLAB])
        xslab = sb("xslab", [P, 2, SLAB])
        hid = sb("hid", [P, 2, 3, 2, SLAB])
        stats = sb("stats", [SLAB, 2, 6])
        mv = sb("mv", [SLAB, 2, 2])
        sd = sb("sd", [SLAB, 2])
        rstd = sb("rstd", [SLAB, 2])
        y_raw = sb("y_raw", [SLAB, 2, P])
        y_sb = sb("y_sb", [SLAB, 2, P])

        gsrc = sb("gsrc", [P, TILES], I32)
        gdst_i = sb("gdst_i", [P, TILES], I32)
        gdst = sb("gdst", [P, TILES])
        gpre = sb("gpre", [P, 2, P])
        goh = sb("goh", [P, CHUNK])
        giota = sb("giota", [P, CHUNK])
        full = sb("full", [P, 2, NCH * CHUNK])

        ps_t = psum("ps_t", [P, 4, GROUP])
        ps_h = psum("ps_h", [P, 2, GROUP])
        ps_m = psum("ps_m", [P, GROUP])
        ps_l = psum("ps_l", [P, GROUP])
        WINDOWS, TURNED, OHT = 0, 1, 2
        ROWS = OHT

        wfirst_in, wrest_in, b_in, dst_in = (sem(k) for k in ("wfirst_in", "wrest_in", "b_in", "dst_in"))
        xt_in = [sem(f"xt_in{k}") for k in range((TBANKS + 1) // 2)]
        iota_done, ident_zero, ident_done = sem("iota_done"), sem("ident_zero"), sem("ident_done")
        ones_done, acc_clear, bias_sum, bias_done = sem("ones_done"), sem("acc_clear"), sem("bias_sum"), sem("bias_done")
        wsrc_mm, wsrc_copied, c_mm, c_copied = sem("wsrc_mm"), sem("wsrc_copied"), sem("c_mm"), sem("c_copied")
        rest_mm, rest_copied, neg_done = sem("rest_mm"), sem("rest_copied"), sem("neg_done")
        ts_mm, ts_copied, ts_stored = sem("ts_mm"), sem("ts_copied"), sem("ts_stored")
        rel_step, bad_done, flag_mm, flag_done = sem("rel_step"), sem("bad_done"), sem("flag_mm"), sem("flag_done")
        idx_in = [sem(f"idx_in{h}") for h in range(2)]
        e_in = [sem(f"e_in{h}") for h in range(2)]
        gathered = [sem(f"gathered{g}") for g in range(GROUPS)]
        x_turned, x_copied = sem("x_turned"), sem("x_copied")
        span_ready, win_mm, win_ready = sem("span_ready"), sem("win_mm"), sem("win_ready")
        oh_ready, oh_turned, oht_ready, ohsum_ready = sem("oh_ready"), sem("oh_turned"), sem("oht_ready"), sem("ohsum_ready")
        pre_done, pre_added, h_ready = sem("pre_done"), sem("pre_added"), sem("h_ready")
        seg_done, acc_added, acc_moved = sem("seg_done"), sem("acc_added"), sem("acc_moved")
        slab_ready, last_added = sem("slab_ready"), sem("last_added")
        xslab_ready, layer_mm, layer_act, stats_done, var_done, sd_done, rstd_done, y_ready, y_out = (
            [sem(f"{k}{lane}") for lane in range(2)] for k in (
                "xslab_ready", "layer_mm", "layer_act", "stats_done", "var_done", "sd_done",
                "rstd_done", "y_ready", "y_out"))
        g_td_mm, g_td_copied, g_td_stored = sem("g_td_mm"), sem("g_td_copied"), sem("g_td_stored")
        g_in, g_dst, g_gath, g_pre = sem("g_in"), sem("g_dst"), sem("g_gath"), sem("g_pre")
        g_added, g_h, g_oh, g_mm, g_acc, g_clear, g_iota = (
            sem(k) for k in ("g_added", "g_h", "g_oh", "g_mm", "g_acc", "g_clear", "g_iota"))

        def W(name):
            return w_sb[:, W_NAMES.index(name), :]

        def B(name, n=1):
            k = B_NAMES.index(name)
            return bc_sb[:, k:k + n]

        def wait(eng, s, value):
            if not isinstance(value, int) or value > 0:
                eng.wait_ge(s, value)

        def after(i, g):
            return (i, g + 1) if g + 1 < GROUPS else (i + 1, 0)

        def chunks(b):
            return range(b * 4, min(b * 4 + 4, TCHUNKS))

        def store_bank(eng, table, b):
            c = slice(chunks(b).start, chunks(b).stop)
            return eng.dma_start(table[c.start * P:c.stop * P, :].rearrange("(c p) f -> p c f", p=P), tab[:, c, :])

        def xt_chunk(c):
            return xt_sb[:, LEFT + c * P:LEFT + (c + 1) * P]

        block = ctx.enter_context(nc.Block())

        @block.sync
        def _(sp):
            def load_idx(i, half):
                for g in (2 * half, 2 * half + 1):
                    wait(sp, gathered[g], 16 * TILES * i)
                c = (i * (GROUPS * TILES)) + half * 2 * TILES
                sp.dma_start(idx[:, half, :], srcT[:, bass.ds(c, 2 * TILES)]).then_inc(idx_in[half], 16)

            def load_e(i, half):
                wait(sp, pre_done, (i - 1) * GROUPS + 2 * half + 2)
                sp.dma_start(lhs[WIN:P, 2 * half:2 * half + 2, :],
                             eT[bass.ds(i * GROUPS + 2 * half, 2)].rearrange("n k c -> k n c")).then_inc(e_in[half], 16)

            def step(i):
                for half in range(2):
                    load_idx(i, half)
                    load_e(i, half)

            load_idx(0, 0)
            sp.dma_start(w_sb[:, 0:W_FIRST, :], weights[:, 0:W_FIRST, :]).then_inc(wfirst_in, 16)
            load_idx(0, 1)
            edges_of_xt = [0] + [LEFT + (k + 1) * 8 * P for k in range(len(xt_in) - 1)] + [COLS]
            for k in range(len(xt_in)):
                c = slice(edges_of_xt[k], edges_of_xt[k + 1])
                sp.dma_start(xt_sb[:, c], xT[:, c]).then_inc(xt_in[k], 16)
            load_e(0, 0)
            load_e(0, 1)
            for b in range(TBANKS):
                sp.wait_ge(ts_copied, b + 1)
                store_bank(sp, table_src, b).then_inc(ts_stored, 16)
            for i in range(1, PEEL):
                step(i)
            with sp.Fori(PEEL, STEPS) as i:
                step(i)

            sp.wait_ge(flag_done, 1)
            wrong = sp.value_load(flag[0:1, 0:1], min_val=0, max_val=NG * GROUP)
            with sp.If(wrong > 0):
                for b in range(TBANKS):
                    sp.wait_ge(g_td_copied, b + 1)
                    store_bank(sp, table_dst, b).then_inc(g_td_stored, 16)

                def general_group(n):
                    wait(sp, g_mm, n * (TILES * NCH))
                    sp.dma_start(gsrc[:, :], srcT[:, bass.ds(n * TILES, TILES)]).then_inc(g_in, 16)
                    sp.dma_start(lhs[WIN:P, 0, :], eT[n]).then_inc(g_in, 16)

                general_group(0)
                with sp.Fori(1, NG) as n:
                    general_group(n)

        @block.gpsimd
        def _(pool):
            bound, nothing = pool.alloc_register("bound"), pool.alloc_register("nothing")
            pool.reg_mov(nothing, 0)

            def gather(i, g, table):
                n = i * GROUPS + g
                if table is x or isinstance(i, int) and i == 1:
                    wait(pool, x_turned, n - GROUPS + 1)
                else:
                    pool.wait_ge(pre_added, n - GROUPS + 1)
                if g % 2 == 0:
                    pool.wait_ge(idx_in[g // 2], (i + 1) * 16)
                pool.reg_add(bound, nothing, NODES - 1)
                for j in range(TILES):
                    col = (g % 2) * TILES + j
                    pool.indirect_dma_start(
                        out=xg[:, g, j * P:(j + 1) * P], out_offset=None, in_=table[:, :],
                        in_offset=bass.IndirectOffsetOnAxis(ap=idx[:, g // 2, col:col + 1], axis=0),
                        bounds_check=bound, oob_is_err=True).then_inc(gathered[g], 16)

            pool.memset(ident[:, :], 0.0).then_inc(ident_zero, 1)
            pool.iota(iota_f[:, :], [[1, WIN]], base=0, channel_multiplier=0,
                      allow_small_or_imprecise_dtypes=True).then_inc(iota_done, 1)
            pool.iota(base_f[:, :], [[SHIFT, NG]], base=0, channel_multiplier=0,
                      allow_small_or_imprecise_dtypes=True).then_inc(iota_done, 1)
            pool.wait_ge(ident_zero, 1)
            pool.affine_select(out=ident[:, :], in_=ident[:, :], compare_op=ALU.not_equal, fill=1.0,
                               base=0, pattern=[[-1, P]], channel_multiplier=1).then_inc(ident_done, 1)
            for g in range(GROUPS):
                gather(0, g, x)
            pool.wait_ge(ts_stored, 16 * TBANKS)
            for i in range(1, PEEL):
                for g in range(GROUPS):
                    gather(i, g, table_src)
            with pool.Fori(PEEL, STEPS) as i:
                for g in range(GROUPS):
                    gather(i, g, table_src)

            pool.wait_ge(flag_done, 1)
            wrong = pool.value_load(flag[0:1, 0:1], min_val=0, max_val=NG * GROUP)
            with pool.If(wrong > 0):
                pool.iota(giota[:, :], [[1, CHUNK]], base=0, channel_multiplier=0,
                          allow_small_or_imprecise_dtypes=True).then_inc(g_iota, 1)

                pool.wait_ge(g_td_stored, 16 * TBANKS)

                def general_gathers(n):
                    pool.wait_ge(g_in, (n + 1) * 32)
                    pool.wait_ge(g_dst, (n + 1) * 2)
                    wait(pool, g_h, n * TILES)
                    pool.reg_add(bound, nothing, TROWS - 1)
                    for side, table, index in ((0, table_src, gsrc), (1, table_dst, gdst_i)):
                        for j in range(TILES):
                            pool.indirect_dma_start(
                                out=xg[:, side, j * P:(j + 1) * P], out_offset=None, in_=table[:, :],
                                in_offset=bass.IndirectOffsetOnAxis(ap=index[:, j:j + 1], axis=0),
                                bounds_check=bound, oob_is_err=True).then_inc(g_gath, 16)

                general_gathers(0)
                with pool.Fori(1, NG) as n:
                    general_gathers(n)

        @block.tensor
        def _(pe):
            pe.wait_ge(wfirst_in, 16)
            pe.matmul(ps_m[:, 0:P], W("WsT"), W("T1"), start=True, stop=True).then_inc(wsrc_mm, 1)
            pe.wait_ge(wsrc_copied, 1)
            for b in range(TBANKS):
                pe.wait_ge(xt_in[b // 2], 16)
                wait(pe, ts_copied, b - 3)
                for c in chunks(b):
                    mm = pe.matmul(ps_t[:, b % 4, (c % 4) * P:(c % 4 + 1) * P], xt_chunk(c), w_src[:, :],
                                   start=True, stop=True)
                mm.then_inc(ts_mm, 1)
                if b == 0:
                    pe.wait_ge(b_in, 48)
                    pe.wait_ge(bias_sum, 2)
                    pe.wait_ge(ones_done, 1)
                    pe.matmul(ps_h[:, 0, 0:P], bsum[:, 1:2].to_broadcast([P, P]), W("T1"), start=True, stop=False)
                    pe.matmul(ps_h[:, 0, 0:P], ones[0:1, :], br_sb[0:1, 0, :], start=False, stop=True).then_inc(c_mm, 1)
                if b == 2:
                    pe.wait_ge(wrest_in, 16)
                    pe.matmul(ps_h[:, 1, P:2 * P], W("WdT"), W("T1"), start=True, stop=True)
                    pe.matmul(ps_h[:, 1, 2 * P:3 * P], W("T2T"), W("Wpe"), start=True, stop=True)
                    pe.matmul(ps_h[:, 1, 3 * P:4 * P], B("tb2").to_broadcast([P, P]), W("Wpe"), start=True, stop=True)
                    pe.matmul(ps_h[WIN:P, 1, 0:P], wet_sb[:, :], W("T1"), start=True, stop=True).then_inc(rest_mm, 1)
            pe.wait_ge(c_copied, 1)
            pe.wait_ge(rest_copied, 4)
            pe.wait_ge(ident_done, 1)
            pe.wait_ge(ts_copied, TBANKS)

            def windows(i):
                pe.wait_ge(span_ready, i + 1)
                wait(pe, win_ready, i)
                for g in range(GROUPS):
                    mm = pe.matmul(ps_t[0:WIN, WINDOWS, g * P:(g + 1) * P], xspan[:, g * SHIFT:g * SHIFT + WIN],
                                   w_dst[:, :], start=True, stop=True)
                mm.then_inc(win_mm, 1)

            def turn_one_hots(i, g):
                n = i * GROUPS + g
                pe.wait_ge(oh_ready, n + 1)
                wait(pe, oht_ready, n - 1)
                for j in range(TILES):
                    mm = pe.transpose(ps_t[0:WIN, OHT + g % 2, j * P:(j + 1) * P], oh[:, g, j, :], ident[:, :])
                mm.then_inc(oh_turned, 1)

            def turn(g):
                pe.wait_ge(gathered[g], 16 * TILES)
                wait(pe, x_copied, g)
                for j in range(TILES):
                    c = slice(j * P, (j + 1) * P)
                    mm = pe.transpose(ps_t[:, TURNED, c], xg[:, g, c], ident[:, :])
                mm.then_inc(x_turned, 1)

            def pre(i, g):
                n = i * GROUPS + g
                pe.wait_ge(oht_ready, n + 1)
                pe.wait_ge(win_ready, i + 1)
                pe.wait_ge(e_in[g // 2], (i + 1) * 16)
                wait(pe, pre_added, n - 1)
                x_rows = isinstance(i, int) and i == 0
                if x_rows:
                    pe.wait_ge(x_copied, g + 1)
                for j in range(TILES):
                    c = slice(j * P, (j + 1) * P)
                    mm = pe.matmul(ps_h[:, g % 2, c], lhs[:, g, c], rhs[:, g, :], start=True, stop=not x_rows)
                    if x_rows:
                        mm = pe.matmul(ps_h[:, g % 2, c], xgt[:, g % 2, c], w_src[:, :], start=False, stop=True)
                mm.then_inc(pre_done, 1)

            def seg(i, g):
                n = i * GROUPS + g
                pe.wait_ge(oh_ready, n + 1)
                wait(pe, acc_added, n)
                pe.wait_ge(h_ready, n + 1)
                for j in range(TILES):
                    mm = pe.matmul(ps_m[:, 0:WIN], h_sb[:, g % 2, j * P:(j + 1) * P], oh[:, g, j, :],
                                   start=(j == 0), stop=(j == TILES - 1))
                mm.then_inc(seg_done, 1)

            def layer(s, k, width=SLAB, lane=0):
                bank = ps_t[:, WINDOWS, :] if lane else ps_l[:, :]
                o = bank[:, 0:width]
                if k == 0:
                    wait(pe, var_done[lane], s)
                    pe.wait_ge(xslab_ready[lane], s + 1)
                    pe.matmul(o, W("Wpd"), xslab[:, lane, 0:width], start=True, stop=False)
                    if lane:
                        pe.wait_ge(acc_added, NG)
                        sums = acc[:, :, END:END + width]
                    else:
                        pe.wait_ge(slab_ready, s + 1)
                        sums = slab[:, :, 0:width]
                    pe.matmul(o, deg_w[:, :], sums[:, 1, :], start=False, stop=False)
                    pe.matmul(o, w_msg[:, :], sums[:, 0, :], start=False, stop=True).then_inc(layer_mm[lane], 1)
                elif k < 3:
                    pe.wait_ge(layer_act[lane], s * 3 + k)
                    mm = pe.matmul(o, W(f"P{k}"), hid[:, lane, k - 1, 0, 0:width], start=True, stop=bool(lane))
                    if not lane:
                        mm = pe.matmul(o, w_neg[:, k - 1, :], hid[:, lane, k - 1, 1, 0:width], start=False, stop=True)
                    mm.then_inc(layer_mm[lane], 1)
                else:
                    o = (ps_t[:, ROWS, :] if lane else bank)[0:width, 0:P]
                    if not lane:
                        pe.wait_ge(layer_act[lane], s * 3 + 3)
                    pe.matmul(o, ones[0:1, 0:width], br_sb[0:1, 1, :], start=True, stop=False)
                    pe.matmul(o, xslab[:, lane, 0:width], ident[:, :], start=False, stop=False)
                    if lane:
                        pe.wait_ge(layer_act[lane], s * 3 + 3)
                    mm = pe.matmul(o, hid[:, lane, 2, 0, 0:width], W("P3"), start=False, stop=bool(lane))
                    if not lane:
                        mm = pe.matmul(o, hid[:, lane, 2, 1, 0:width], w_neg[:, 2, :], start=False, stop=True)
                    mm.then_inc(layer_mm[lane], 1)

            def step(i, k, last=False):
                for g in range(GROUPS):
                    if k == 0:
                        turn(g)
                    else:
                        pre(i, g)
                    if not (last and g == GROUPS - 1):
                        if g == GROUPS - 1:
                            windows(i + 1)
                        turn_one_hots(*after(i, g))
                    if k == 0:
                        pre(i, g)
                    if g >= 2 and k >= 1:
                        layer(i - 1, 2 * (g - 2))
                    if g >= 1:
                        seg(i, g - 1)
                    elif k >= 1:
                        seg(i - 1, GROUPS - 1)
                    if g >= 2 and k >= 1:
                        layer(i - 1, 2 * (g - 2) + 1)

            windows(0)
            turn_one_hots(0, 0)
            step(0, 0)
            pe.wait_ge(neg_done, 1)
            for i in range(1, PEEL):
                step(i, i)
            pe.wait_ge(bad_done, 1)
            pe.matmul(ps_t[0:1, TURNED, 0:1], badsum[:, :], ones[:, 0:1], start=True, stop=True).then_inc(flag_mm, 1)
            with pe.Fori(PEEL, STEPS - 1) as i:
                step(i, PEEL)
            step(STEPS - 1, PEEL, True)
            layer(STEPS - 1, 0, END)
            seg(STEPS - 1, GROUPS - 1)
            for k in range(1, 4):
                layer(STEPS - 1, k, END)
                layer(0, k - 1, TAIL, 1)
            layer(0, 3, TAIL, 1)

            pe.wait_ge(flag_done, 1)
            wrong = pe.value_load(flag[0:1, 0:1], min_val=0, max_val=NG * GROUP)
            with pe.If(wrong > 0):
                pe.wait_ge(var_done[1], 1)
                for b in range(TBANKS):
                    wait(pe, g_td_copied, b - 1)
                    for c in chunks(b):
                        mm = pe.matmul(ps_t[:, b % 2, (c % 4) * P:(c % 4 + 1) * P], xt_chunk(c), w_dst[:, :],
                                       start=True, stop=True)
                    mm.then_inc(g_td_mm, 1)
                pe.wait_ge(g_td_copied, TBANKS)

                def general_group(n):
                    pe.wait_ge(g_in, (n + 1) * 32)
                    for j in range(TILES):
                        m = n * TILES + j
                        wait(pe, g_h, m)
                        pe.matmul(ps_h[:, 0, 0:P], lhs[WIN:P, 0, j * P:(j + 1) * P], rhs[WIN:P, 0, :],
                                  start=True, stop=True).then_inc(g_pre, 1)
                        pe.wait_ge(g_h, m + 1)
                        for c in range(NCH):
                            q = m * NCH + c
                            wait(pe, g_acc, q)
                            pe.wait_ge(g_oh, q + 1)
                            pe.matmul(ps_t[:, 0, :], h_sb[:, 0, 0:P], goh[:, :], start=True, stop=True).then_inc(g_mm, 1)

                general_group(0)
                with pe.Fori(1, NG) as n:
                    general_group(n)
                with pe.Fori(0, STEPS) as s:
                    for k in range(4):
                        layer(s + STEPS, k)
                for k in range(4):
                    layer(2 * STEPS, k, TAIL)

        @block.scalar
        def _(act):
            act.dma_start(dst_i[:, :], dstT).then_inc(dst_in, 16)
            act.dma_start(bc_sb[:, :], bcols).then_inc(b_in, 16)
            act.dma_start(br_sb[:, :, :], brows).then_inc(b_in, 16)
            act.dma_start(wet_sb[:, :], WeT).then_inc(b_in, 16)
            act.dma_start(w_sb[:, W_FIRST:, :], weights[:, W_FIRST:, :]).then_inc(wrest_in, 16)

            def copy_span(i):
                wait(act, win_mm, i)
                act.activation(xspan[:, :], xt_sb[:, bass.ds(i * SLAB, SPAN)], ACT.Copy).then_inc(span_ready, 1)

            def copy_windows(i):
                act.wait_ge(win_mm, i + 1)
                wait(act, pre_done, i * GROUPS)
                act.activation(rhs[0:WIN, :, :].rearrange("w g f -> w (g f)"), ps_t[0:WIN, WINDOWS, :],
                               ACT.Copy).then_inc(win_ready, 1)

            def copy_one_hots(i, g):
                n = i * GROUPS + g
                act.wait_ge(oh_turned, n + 1)
                wait(act, pre_done, n - GROUPS + 1)
                act.activation(lhs[0:WIN, g, :], ps_t[0:WIN, OHT + g % 2, :], ACT.Copy).then_inc(oht_ready, 1)

            def copy_turned(g):
                act.wait_ge(x_turned, g + 1)
                wait(act, pre_done, g - 1)
                act.activation(xgt[:, g % 2, :], ps_t[:, TURNED, :], ACT.Copy).then_inc(x_copied, 1)

            def copy_xslab(s, col, width=SLAB, lane=0):
                wait(act, layer_mm[lane], s * 4)
                act.activation(xslab[:, lane, 0:width], xt_sb[:, bass.ds(col, width)], ACT.Copy).then_inc(xslab_ready[lane], 1)

            def close_slab(s):
                act.wait_ge(acc_added, (s + 1) * GROUPS)
                wait(act, layer_mm[0], s * 4)
                act.activation(slab[:, :, :], acc[:, :, 0:SLAB], ACT.Copy).then_inc(slab_ready, 1)
                act.wait_ge(slab_ready, s + 1)
                act.activation(acc[:, :, 0:SPAN - SLAB], acc[:, :, SLAB:SPAN], ACT.Copy).then_inc(acc_moved, 1)

            def layer_out(s, k, width=SLAB):
                act.wait_ge(layer_mm[0], s * 4 + (k + 1))
                act.activation(hid[:, 0, k, 0, 0:width], ps_l[:, 0:width], ACT.Relu, bias=bias[:, 0, k:k + 1])
                act.activation(hid[:, 0, k, 1, 0:width], ps_l[:, 0:width], ACT.Relu, bias=bias[:, 1, k:k + 1],
                               scale=-1.0).then_inc(layer_act[0], 1)

            def deviation(s, width=SLAB, lane=0):
                act.wait_ge(var_done[lane], s + 1)
                act.activation(sd[0:width, lane:lane + 1], mv[0:width, lane, 1:2], ACT.Sqrt,
                               bias=eps_sb[0:width, :]).then_inc(sd_done[lane], 1)

            def store(s, row, width=SLAB, lane=0):
                act.wait_ge(y_ready[lane], s + 1)
                act.dma_start(out[bass.ds(row, width), :], y_sb[0:width, lane, :]).then_inc(y_out[lane], 16)

            def step(i, k, last=False):
                for g in range(GROUPS):
                    if k == 0:
                        copy_turned(g)
                    if not (last and g == GROUPS - 1):
                        if g == GROUPS - 1:
                            copy_windows(i + 1)
                        copy_one_hots(*after(i, g))
                    if g == 2 and not last:
                        copy_span(i + 1)
                    if g == 0 and k >= 2:
                        deviation(i - 2)
                    if g == 1 and k >= 2:
                        store(i - 2, (i - 2) * SLAB)
                    if g == 1 and k >= 1:
                        copy_xslab(i - 1, (i - 1) * SLAB)
                        close_slab(i - 1)
                    if g == 2 and k >= 1:
                        layer_out(i - 1, 0)
                        layer_out(i - 1, 1)
                    if g == 3 and k >= 1:
                        layer_out(i - 1, 2)

            act.wait_ge(rest_mm, 1)
            act.activation(w_dst[:, :], ps_h[:, 1, P:2 * P], ACT.Copy).then_inc(rest_copied, 1)
            act.activation(w_msg[:, :], ps_h[:, 1, 2 * P:3 * P], ACT.Copy).then_inc(rest_copied, 1)
            act.activation(deg_w[:, :], ps_h[:, 1, 3 * P:4 * P], ACT.Copy).then_inc(rest_copied, 1)
            act.activation(rhs[WIN:P, :, :], ps_h[WIN:P, 1, None, 0:P].to_broadcast([EDIM, GROUPS, P]),
                           ACT.Copy).then_inc(rest_copied, 1)
            act.wait_ge(xt_in[0], 16)
            copy_span(0)
            copy_windows(0)
            copy_one_hots(0, 0)
            step(0, 0)
            for s in xt_in[1:]:
                act.wait_ge(s, 16)
            act.wait_ge(bias_done, 3)
            for i in range(1, PEEL):
                step(i, i)
            with act.Fori(PEEL, STEPS - 1) as i:
                step(i, PEEL)
            step(STEPS - 1, PEEL, True)
            copy_xslab(STEPS - 1, (STEPS - 1) * SLAB, END)
            copy_xslab(0, LAST, TAIL, 1)
            deviation(STEPS - 2)
            layer_out(STEPS - 1, 0, END)
            store(STEPS - 2, (STEPS - 2) * SLAB)
            layer_out(STEPS - 1, 1, END)
            layer_out(STEPS - 1, 2, END)
            deviation(STEPS - 1, END)
            store(STEPS - 1, (STEPS - 1) * SLAB, END)
            deviation(0, TAIL, 1)
            store(0, LAST, TAIL, 1)
            act.wait_ge(y_out[0], 16 * STEPS)
            act.wait_ge(y_out[1], 16)

            act.wait_ge(flag_done, 1)
            wrong = act.value_load(flag[0:1, 0:1], min_val=0, max_val=NG * GROUP)
            with act.If(wrong > 0):
                def general_slab(s, col, width=SLAB):
                    copy_xslab(s, col, width)
                    for k in range(3):
                        layer_out(s, k, width)
                    deviation(s, width)
                    store(s, col, width)

                with act.Fori(0, STEPS) as s:
                    general_slab(s + STEPS, s * SLAB)
                general_slab(2 * STEPS, LAST, TAIL)
                act.wait_ge(y_out[0], 16 * (STEPS + SLABS))

        @block.vector
        def _(dve):
            dve.memset(ones[:, :], 1.0).then_inc(ones_done, 1)
            dve.memset(eps_sb[:, :], EPS)
            dve.memset(acc[:, :, :], 0.0).then_inc(acc_clear, 1)
            dve.wait_ge(iota_done, 2)
            dve.wait_ge(dst_in, 16)
            dve.tensor_scalar(dst_f[:, :], dst_i[:, :], float(LEFT), None, ALU.add).then_inc(rel_step, 1)
            dve.wait_ge(rel_step, 1)
            dve.tensor_tensor(rel[:, :, :], dst_f[:, :].rearrange("p (n j) -> p n j", j=TILES),
                              base_f[:, :, None].to_broadcast([P, NG, TILES]), ALU.subtract).then_inc(rel_step, 1)
            dve.wait_ge(wsrc_mm, 1)
            dve.tensor_copy(w_src[:, :], ps_m[:, 0:P]).then_inc(wsrc_copied, 1)
            def layer_constants():
                dve.tensor_tensor(bias[:, 0, 0:1], B("bpd"), B("bpe"), ALU.add).then_inc(bias_done, 1)
                dve.tensor_copy(bias[:, 0, 1:3], B("pb1", 2)).then_inc(bias_done, 1)
                dve.wait_ge(wrest_in, 16)
                dve.tensor_scalar(w_neg[:, :, :], w_sb[:, W_NAMES.index("P1"):, :], -SLOPE, None, ALU.mult).then_inc(neg_done, 1)
                dve.wait_ge(bias_done, 2)
                dve.tensor_scalar(bias[:, 1, :], bias[:, 0, :], -1.0, None, ALU.mult).then_inc(bias_done, 1)

            def count_bad():
                relv = rel[:, :, :].rearrange("p n j -> p (n j)")
                dve.tensor_scalar(bad[:, :], relv, 0.0, None, ALU.is_lt).then_inc(rel_step, 1)
                dve.wait_ge(rel_step, 3)
                dve.scalar_tensor_tensor(out=bad[:, :], in0=relv, scalar=float(WIN - 1), in1=bad[:, :],
                                         op0=ALU.is_gt, op1=ALU.add).then_inc(rel_step, 1)
                dve.wait_ge(rel_step, 4)
                dve.tensor_reduce(badsum[:, :], bad[:, :], AX.X, ALU.add).then_inc(bad_done, 1)

            def one_hots(i, g):
                n = i * GROUPS + g
                wait(dve, seg_done, n - GROUPS + 1)
                dve.tensor_tensor(
                    oh[:, g, :, :], iota_f[:, None, 0:WIN].to_broadcast([P, TILES, WIN]),
                    rel[:, bass.ds(n, 1), :].rearrange("p a j -> p (a j)")[:, :, None].to_broadcast([P, TILES, WIN]),
                    ALU.is_equal).then_inc(oh_ready, 1)
                dve.wait_ge(oh_ready, n + 1)
                dve.tensor_reduce(ohsum[:, g, :], oh[:, g, :, :].rearrange("p j w -> p w j"), AX.X,
                                  ALU.add).then_inc(ohsum_ready, 1)

            def hidden(i, g):
                n = i * GROUPS + g
                dve.wait_ge(pre_done, n + 1)
                dve.wait_ge(gathered[g], (i + 1) * (16 * TILES))
                wait(dve, h_ready, n)
                if isinstance(i, int) and i == 0:
                    dve.tensor_tensor(h_pre[:, :].rearrange("p (j f) -> p j f", j=TILES),
                                      ps_h[:, g % 2, :].rearrange("p (j f) -> p j f", j=TILES),
                                      c_rows[:, None, :].to_broadcast([P, TILES, P]), ALU.add).then_inc(pre_added, 1)
                else:
                    dve.tensor_tensor(h_pre[:, :], ps_h[:, g % 2, :], xg[:, g, :], ALU.add).then_inc(pre_added, 1)
                dve.wait_ge(pre_added, n + 1)
                wait(dve, seg_done, n - 1)
                dve.scalar_tensor_tensor(out=h_sb[:, g % 2, :], in0=h_pre[:, :], scalar=SLOPE, in1=h_pre[:, :],
                                         op0=ALU.mult, op1=ALU.max).then_inc(h_ready, 1)

            def add_sums(i, g, moves):
                n = i * GROUPS + g
                wait(dve, acc_moved, moves * 2)
                wait(dve, acc_added, n)
                dve.wait_ge(ohsum_ready, n + 1)
                o = g * SHIFT
                dve.tensor_tensor(acc[:, 1, o:o + WIN], acc[:, 1, o:o + WIN], ohsum[:, g, :], ALU.add)
                dve.wait_ge(seg_done, n + 1)
                dve.tensor_tensor(acc[:, 0, o:o + WIN], acc[:, 0, o:o + WIN], ps_m[:, 0:WIN], ALU.add).then_inc(acc_added, 1)

            def clear_sums(s):
                dve.wait_ge(acc_moved, s * 2 + 1)
                dve.memset(acc[:, :, SPAN - SLAB:SPAN], 0.0).then_inc(acc_moved, 1)

            def hand_on(s, groups, width):
                dve.wait_ge(acc_added, groups)
                wait(dve, layer_mm[0], s * 4)
                dve.tensor_copy(slab[:, :, 0:width], acc[:, :, 0:width]).then_inc(slab_ready, 1)

            def last_layer_out(k):
                dve.wait_ge(layer_mm[1], k + 1)
                total = hid[:, 1, k, 1, 0:TAIL]
                dve.tensor_scalar(total, ps_t[:, WINDOWS, 0:TAIL], bias[:, 0, k:k + 1], None, ALU.add).then_inc(last_added, 1)
                dve.wait_ge(last_added, k + 1)
                dve.scalar_tensor_tensor(out=hid[:, 1, k, 0, 0:TAIL], in0=total, scalar=SLOPE, in1=total,
                                         op0=ALU.mult, op1=ALU.max).then_inc(layer_act[1], 1)

            def statistics(s, width=SLAB, lane=0):
                y = ps_t[0:width, ROWS, 0:P] if lane else ps_l[0:width, 0:P]
                dve.wait_ge(layer_mm[lane], s * 4 + 4)
                dve.bn_stats(stats[0:width, lane, :], y).then_inc(stats_done[lane], 1)
                dve.wait_ge(stats_done[lane], s + 1)
                dve.tensor_copy(y_raw[0:width, lane, :], y)
                dve.bn_aggr(mv[0:width, lane, :], stats[0:width, lane, :]).then_inc(var_done[lane], 1)

            def normalize(s, width=SLAB, lane=0):
                dve.wait_ge(sd_done[lane], s + 1)
                dve.reciprocal(rstd[0:width, lane:lane + 1], sd[0:width, lane:lane + 1]).then_inc(rstd_done[lane], 1)
                wait(dve, y_out[lane], s * 16)
                dve.wait_ge(rstd_done[lane], s + 1)
                dve.tensor_scalar(y_sb[0:width, lane, :], y_raw[0:width, lane, :], mv[0:width, lane, 0:1],
                                  rstd[0:width, lane:lane + 1], ALU.subtract, ALU.mult).then_inc(y_ready[lane], 1)

            def step(i, k, last=False):
                for g in range(GROUPS):
                    if not (last and g == GROUPS - 1):
                        one_hots(*after(i, g))
                    if g == 1 and k >= 2:
                        normalize(i - 2)
                    if g >= 1:
                        hidden(i, g - 1)
                    elif k >= 1:
                        hidden(i - 1, GROUPS - 1)
                    if g == 0 and k >= 2:
                        statistics(i - 2)
                    if g == 2 and k >= 1:
                        clear_sums(i - 1)
                    if g >= 2:
                        add_sums(i, g - 2, i)
                    elif k >= 1:
                        add_sums(i - 1, g + GROUPS - 2, i - 1)

            dve.wait_ge(b_in, 48)
            dve.tensor_tensor(bsum[:, 0:1], B("be"), B("bs"), ALU.add).then_inc(bias_sum, 1)
            dve.wait_ge(bias_sum, 1)
            dve.tensor_tensor(bsum[:, 1:2], bsum[:, 0:1], B("bd"), ALU.add).then_inc(bias_sum, 1)
            dve.wait_ge(c_mm, 1)
            dve.tensor_copy(c_rows[:, :], ps_h[:, 0, 0:P]).then_inc(c_copied, 1)
            dve.wait_ge(c_copied, 1)
            dve.wait_ge(rel_step, 2)
            one_hots(0, 0)
            for b in range(TBANKS):
                n = len(chunks(b))
                dve.wait_ge(ts_mm, b + 1)
                dve.tensor_tensor(tab[:, b * 4:b * 4 + n, :], ps_t[:, b % 4, 0:n * P].rearrange("p (c f) -> p c f", c=n),
                                  c_rows[:, None, :].to_broadcast([P, n, P]), ALU.add).then_inc(ts_copied, 1)
            dve.wait_ge(acc_clear, 1)
            step(0, 0)
            layer_constants()
            count_bad()
            for i in range(1, PEEL):
                step(i, i)
            with dve.Fori(PEEL, STEPS - 1) as i:
                step(i, PEEL)
            step(STEPS - 1, PEEL, True)
            add_sums(STEPS - 1, GROUPS - 2, STEPS - 1)
            hand_on(STEPS - 1, NG - 1, END)
            statistics(STEPS - 2)
            hidden(STEPS - 1, GROUPS - 1)
            normalize(STEPS - 2)
            add_sums(STEPS - 1, GROUPS - 1, STEPS - 1)
            last_layer_out(0)
            last_layer_out(1)
            statistics(STEPS - 1, END)
            last_layer_out(2)
            normalize(STEPS - 1, END)
            dve.wait_ge(flag_mm, 1)
            dve.tensor_copy(flag[:, :], ps_t[0:1, TURNED, 0:1]).then_inc(flag_done, 1)
            statistics(0, TAIL, 1)
            normalize(0, TAIL, 1)

            dve.wait_ge(flag_done, 1)
            wrong = dve.value_load(flag[0:1, 0:1], min_val=0, max_val=NG * GROUP)
            with dve.If(wrong > 0):
                for b in range(TBANKS):
                    n = len(chunks(b))
                    dve.wait_ge(g_td_mm, b + 1)
                    dve.tensor_copy(tab[:, b * 4:b * 4 + n, :].rearrange("p c f -> p (c f)"),
                                    ps_t[:, b % 2, 0:n * P]).then_inc(g_td_copied, 1)
                dve.memset(full[:, :, :], 0.0).then_inc(g_clear, 1)
                dve.wait_ge(g_clear, 1)
                dve.wait_ge(g_iota, 1)

                def general_group(n):
                    wait(dve, g_mm, n * (TILES * NCH))
                    dve.tensor_copy(gdst[:, :], dst_f[:, bass.ds(n * TILES, TILES)]).then_inc(g_dst, 1)
                    dve.tensor_copy(gdst_i[:, :], dst_i[:, bass.ds(n * TILES, TILES)]).then_inc(g_dst, 1)
                    dve.wait_ge(g_dst, (n + 1) * 2)
                    dve.wait_ge(g_gath, (n + 1) * (32 * TILES))
                    for j in range(TILES):
                        m = n * TILES + j
                        c = slice(j * P, (j + 1) * P)
                        dve.wait_ge(g_pre, m + 1)
                        dve.tensor_tensor(gpre[:, 0, :], ps_h[:, 0, 0:P], xg[:, 0, c], ALU.add).then_inc(g_added, 1)
                        dve.wait_ge(g_added, m * 2 + 1)
                        dve.tensor_tensor(gpre[:, 1, :], gpre[:, 0, :], xg[:, 1, c], ALU.add).then_inc(g_added, 1)
                        wait(dve, g_mm, m * NCH)
                        dve.wait_ge(g_added, m * 2 + 2)
                        dve.scalar_tensor_tensor(out=h_sb[:, 0, 0:P], in0=gpre[:, 1, :], scalar=SLOPE, in1=gpre[:, 1, :],
                                                 op0=ALU.mult, op1=ALU.max).then_inc(g_h, 1)
                        for k in range(NCH):
                            q = m * NCH + k
                            wait(dve, g_mm, q)
                            wait(dve, g_acc, q)
                            dve.tensor_scalar(goh[:, :], giota[:, :], float(CHUNK * k), gdst[:, j:j + 1],
                                              ALU.add, ALU.is_equal).then_inc(g_oh, 1)
                            dve.wait_ge(g_oh, q + 1)
                            part = slice(k * CHUNK, (k + 1) * CHUNK)
                            dve.tensor_tensor(full[:, 1, part], full[:, 1, part], goh[:, :], ALU.add)
                            dve.wait_ge(g_mm, q + 1)
                            dve.tensor_tensor(full[:, 0, part], full[:, 0, part], ps_t[:, 0, :], ALU.add).then_inc(g_acc, 1)

                general_group(0)
                with dve.Fori(1, NG) as n:
                    general_group(n)
                dve.wait_ge(g_acc, NG * TILES * NCH)

                def general_slab(s, col, width=SLAB):
                    dve.wait_ge(layer_mm[0], s * 4)
                    dve.tensor_copy(slab[:, :, 0:width], full[:, :, bass.ds(col, width)]).then_inc(slab_ready, 1)
                    statistics(s, width)
                    normalize(s, width)

                with dve.Fori(0, STEPS) as s:
                    general_slab(s + STEPS, s * SLAB)
                general_slab(2 * STEPS, LAST, TAIL)


def kernel(**inputs):
    import numpy as np
    import concourse.bacc as bacc
    from concourse.bass_utils import run_bass_kernel_spmd as run

    a = {k.replace("L0_gnn_", ""): np.ascontiguousarray(v) for k, v in inputs.items()}
    padded = NG * GROUP

    def edges(v, fill):
        full = np.full((padded,) + v.shape[1:], fill, v.dtype)
        full[:EDGES] = v
        return full.reshape((NG, P, TILES) + v.shape[1:])

    xT = np.zeros((P, COLS), a["x"].dtype)
    xT[:, LEFT:LEFT + NODES] = a["x"].T
    a["WsT"], a["WdT"], a["T2T"] = a["Ws"].T, a["Wd"].T, a["T2"].T
    arrays = {
        "x": a["x"],
        "xT": xT,
        "srcT": edges(a["src"], 0).transpose(1, 0, 2).reshape(P, -1),
        "dstT": edges(a["dst"], NODES).transpose(1, 0, 2).reshape(P, -1),
        "eT": edges(a["edge_attr_32"], 0).transpose(0, 3, 2, 1).reshape(NG, EDIM, GROUP),
        "weights": np.stack([a[k] for k in W_NAMES], axis=1),
        "WeT": a["We"].T,
        "bcols": np.stack([a[k] for k in B_NAMES], axis=1),
        "brows": np.stack([a["tb1"], a["pb3"]])[None],
    }
    nc = bacc.Bacc("TRN2", target_bir_lowering=False, num_devices=1)
    feed, args = {}, []
    for name, v in arrays.items():
        feed[f"in_{name}"] = np.ascontiguousarray(v)
        args.append(nc.dram_tensor(f"in_{name}", v.shape, mybir.dt.from_np(v.dtype), kind="ExternalInput").ap())
    args.append(nc.dram_tensor("out_rows", (OUT_ROWS, P), F32, kind="ExternalOutput").ap())
    gnn_resnorm(nc, *args)
    r = run(nc, [feed], core_ids=[0])
    return r.results[0]["out_rows"][LEFT:LEFT + NODES]
```
